# Optimizing a Trainium2 kernel written in Bass

```python
import numpy as np
import jax
import jax.numpy as jnp

def _softmax(x, axis=-1):
    return jax.nn.softmax(x, axis=axis)

def _gelu(x):
    return jax.nn.gelu(x, approximate=True)

def _silu(x):
    return jax.nn.silu(x)

def _sigmoid(x):
    return jax.nn.sigmoid(x)

def _layernorm(x, axis=-1, eps=1e-05):
    m = jnp.mean(x, axis=axis, keepdims=True)
    v = jnp.var(x, axis=axis, keepdims=True)
    return (x - m) / jnp.sqrt(v + eps)

def _scatter_add(tgt, idx, src, axis=0):
    return tgt.at[idx].add(src)

def _segment_sum(src, seg, n):
    return jax.ops.segment_sum(src, seg, n)
kernel_name = 'mk_vit_tower_cls_d1_tok_img256_r4_650479'

def setup_inputs(seed: int=0):
    np.random.seed(seed)
    _w = jnp.asarray

    def _rec_inputs():
        import jax
        import jax.numpy as jnp
        _rk = jax.random.key(seed)
        x = 7.22013e-05 + 1.00017 * jax.random.normal(jax.random.fold_in(_rk, 1), (4, 64, 64, 64), jnp.float32)
        cls_tok = 0.02 * jax.random.normal(jax.random.fold_in(_rk, 5), (1, 1, 64), jnp.float32)
        return (x, cls_tok)
    x, cls_tok = _rec_inputs()

    def _L0_tok_setup():
        import jax, jax.numpy as jnp
        import numpy as np
        K = 3
        PAD = (K - 1) // 2
        BN_EPS = 1e-05

        def _unfold(x):
            b, c, h, w = x.shape
            xp = jnp.pad(x, ((0, 0), (0, 0), (PAD, PAD), (PAD, PAD)))
            shifts = [xp[:, :, i:i + h, j:j + w] for i in range(K) for j in range(K)]
            return jnp.stack(shifts, axis=2)
        key = jax.random.key(seed)
        ks = jax.random.split(key, 4)
        b, c, h, w = (8, 64, 64, 64)
        cr = c // 4
        x = jax.random.normal(ks[0], (b, c, h, w), dtype=jnp.float32)
        conv1_w = jax.random.normal(ks[1], (cr, c), dtype=jnp.float32) * (1.0 / np.sqrt(c))
        conv1_b = jnp.zeros((cr,), dtype=jnp.float32)
        bn_gamma = jnp.ones((cr,), dtype=jnp.float32)
        bn_beta = jnp.zeros((cr,), dtype=jnp.float32)
        bn_mean = jnp.zeros((cr,), dtype=jnp.float32)
        bn_var = jnp.ones((cr,), dtype=jnp.float32)
        conv2_w = jax.random.normal(ks[2], (K * K, cr), dtype=jnp.float32) * (1.0 / np.sqrt(cr))
        conv2_b = jnp.zeros((K * K,), dtype=jnp.float32)
        return {'x': x, 'conv1_w': conv1_w, 'conv1_b': conv1_b, 'bn_gamma': bn_gamma, 'bn_beta': bn_beta, 'bn_mean': bn_mean, 'bn_var': bn_var, 'conv2_w': conv2_w, 'conv2_b': conv2_b}
    _L0_tok_all = _L0_tok_setup()
    _L0_tok_in = {k: v for k, v in _L0_tok_all.items() if k in ('conv1_w', 'conv1_b', 'bn_gamma', 'bn_beta', 'bn_mean', 'bn_var', 'conv2_w', 'conv2_b')}
    del _L0_tok_all

    def _L0_attn_setup():
        import jax, jax.numpy as jnp
        import numpy as np
        GAMMA = 0.96875
        SCALE_BASE = 512.0

        def xpos_rope(x, downscale=False):
            B, S, D = x.shape
            half = D // 2
            inv_freq = 1.0 / 10000.0 ** (jnp.arange(0, D, 2, dtype=jnp.float32) / D)
            pos = jnp.arange(S, dtype=jnp.float32)
            ang = pos[:, None] * inv_freq[None, :]
            sin, cos = (jnp.sin(ang), jnp.cos(ang))
            base = (jnp.arange(0, D, 2, dtype=jnp.float32) + 0.4 * D) / (1.4 * D)
            scale = base[None, :] ** (pos[:, None] / SCALE_BASE)
            if downscale:
                scale = 1.0 / scale
            x1 = x[..., 0::2]
            x2 = x[..., 1::2]
            r1 = (x1 * cos - x2 * sin) * scale
            r2 = (x1 * sin + x2 * cos) * scale
            out = jnp.stack([r1, r2], axis=-1).reshape(B, S, D)
            return out

        def get_D(gamma, seq_len):
            n = jnp.arange(seq_len, dtype=jnp.float32)
            diff = n[:, None] - n[None, :]
            mask = diff >= 0
            D = jnp.where(mask, gamma ** jnp.where(mask, diff, 0.0), 0.0)
            return D

        def _reference_tuple_inner(x, W_Q, W_K, W_V):
            S = x.shape[1]
            D = get_D(GAMMA, S)
            Q = xpos_rope(x @ W_Q, downscale=False)
            K = xpos_rope(x @ W_K, downscale=True)
            V = x @ W_V
            ret = jnp.einsum('bnd,bmd->bnm', Q, K) * D[None, :, :]
            out = jnp.einsum('bnm,bmv->bnv', ret, V)
            return (out, ret)
        key = jax.random.key(seed)
        k1, k2, k3, k4 = jax.random.split(key, 4)
        B, S, d_model, d_k, d_v = (8, 1024, 64, 64, 64)
        x = jax.random.normal(k1, (B, S, d_model), dtype=jnp.float32)
        W_Q = jax.random.normal(k2, (d_model, d_k), dtype=jnp.float32) / d_model
        W_K = jax.random.normal(k3, (d_model, d_k), dtype=jnp.float32) / d_model
        W_V = jax.random.normal(k4, (d_model, d_v), dtype=jnp.float32) / d_model
        return {'x': x, 'W_Q': W_Q, 'W_K': W_K, 'W_V': W_V}
    _L0_attn_all = _L0_attn_setup()
    _L0_attn_in = {k: v for k, v in _L0_attn_all.items() if k in ('W_Q', 'W_K', 'W_V')}
    del _L0_attn_all

    def _L0_ffn_setup():
        import jax, jax.numpy as jnp
        import numpy as np
        B, S, D, E, H, K = (4, 1024, 64, 8, 128, 2)
        key = jax.random.key(seed)
        ks = jax.random.split(key, 6)
        x = jax.random.normal(ks[0], (B, S, D), jnp.float32)
        Wg = jax.random.normal(ks[1], (D, E), jnp.float32) * 0.02
        bg = jnp.zeros((E,), jnp.float32)
        W1 = jax.random.normal(ks[2], (E, D, H), jnp.float32) * 0.02
        b1 = jnp.zeros((E, H), jnp.float32)
        W2 = jax.random.normal(ks[3], (E, H, D), jnp.float32) * 0.02
        b2 = jnp.zeros((E, D), jnp.float32)
        return {'x': x, 'Wg': Wg, 'bg': bg, 'W1': W1, 'b1': b1, 'W2': W2, 'b2': b2}
    _L0_ffn_all = _L0_ffn_setup()
    _L0_ffn_in = {k: v for k, v in _L0_ffn_all.items() if k in ('Wg', 'bg', 'W1', 'b1', 'W2', 'b2')}
    del _L0_ffn_all
    return {'x': x, 'cls_tok': cls_tok, 'L0_tok_conv1_w': _L0_tok_in['conv1_w'], 'L0_tok_conv1_b': _L0_tok_in['conv1_b'], 'L0_tok_bn_gamma': _L0_tok_in['bn_gamma'], 'L0_tok_bn_beta': _L0_tok_in['bn_beta'], 'L0_tok_bn_mean': _L0_tok_in['bn_mean'], 'L0_tok_bn_var': _L0_tok_in['bn_var'], 'L0_tok_conv2_w': _L0_tok_in['conv2_w'], 'L0_tok_conv2_b': _L0_tok_in['conv2_b'], 'L0_attn_W_Q': _L0_attn_in['W_Q'], 'L0_attn_W_K': _L0_attn_in['W_K'], 'L0_attn_W_V': _L0_attn_in['W_V'], 'L0_ffn_Wg': _L0_ffn_in['Wg'], 'L0_ffn_bg': _L0_ffn_in['bg'], 'L0_ffn_W1': _L0_ffn_in['W1'], 'L0_ffn_b1': _L0_ffn_in['b1'], 'L0_ffn_W2': _L0_ffn_in['W2'], 'L0_ffn_b2': _L0_ffn_in['b2']}

def reference(x, cls_tok, L0_tok_conv1_w, L0_tok_conv1_b, L0_tok_bn_gamma, L0_tok_bn_beta, L0_tok_bn_mean, L0_tok_bn_var, L0_tok_conv2_w, L0_tok_conv2_b, L0_attn_W_Q, L0_attn_W_K, L0_attn_W_V, L0_ffn_Wg, L0_ffn_bg, L0_ffn_W1, L0_ffn_b1, L0_ffn_W2, L0_ffn_b2):
    import jax
    import jax.numpy as jnp

    def _L0_tok_ref(x, conv1_w, conv1_b, bn_gamma, bn_beta, bn_mean, bn_var, conv2_w, conv2_b):
        import jax, jax.numpy as jnp
        import numpy as np
        K = 3
        PAD = (K - 1) // 2
        BN_EPS = 1e-05

        def _unfold(x):
            b, c, h, w = x.shape
            xp = jnp.pad(x, ((0, 0), (0, 0), (PAD, PAD), (PAD, PAD)))
            shifts = [xp[:, :, i:i + h, j:j + w] for i in range(K) for j in range(K)]
            return jnp.stack(shifts, axis=2)
        b, c, h, w = x.shape
        y = jnp.einsum('oc,bchw->bohw', conv1_w, x) + conv1_b[None, :, None, None]
        y = (y - bn_mean[None, :, None, None]) * (bn_gamma[None, :, None, None] * jax.lax.rsqrt(bn_var + BN_EPS)[None, :, None, None]) + bn_beta[None, :, None, None]
        y = jax.nn.relu(y)
        wdyn = jnp.einsum('ok,bkhw->bohw', conv2_w, y) + conv2_b[None, :, None, None]
        patches = _unfold(x)
        out = jnp.einsum('bckhw,bkhw->bchw', patches, wdyn)
        return out.reshape(b, h * w, c)

    def _L0_attn_ref(x, W_Q, W_K, W_V):
        import jax, jax.numpy as jnp
        import numpy as np
        GAMMA = 0.96875
        SCALE_BASE = 512.0

        def xpos_rope(x, downscale=False):
            B, S, D = x.shape
            half = D // 2
            inv_freq = 1.0 / 10000.0 ** (jnp.arange(0, D, 2, dtype=jnp.float32) / D)
            pos = jnp.arange(S, dtype=jnp.float32)
            ang = pos[:, None] * inv_freq[None, :]
            sin, cos = (jnp.sin(ang), jnp.cos(ang))
            base = (jnp.arange(0, D, 2, dtype=jnp.float32) + 0.4 * D) / (1.4 * D)
            scale = base[None, :] ** (pos[:, None] / SCALE_BASE)
            if downscale:
                scale = 1.0 / scale
            x1 = x[..., 0::2]
            x2 = x[..., 1::2]
            r1 = (x1 * cos - x2 * sin) * scale
            r2 = (x1 * sin + x2 * cos) * scale
            out = jnp.stack([r1, r2], axis=-1).reshape(B, S, D)
            return out

        def get_D(gamma, seq_len):
            n = jnp.arange(seq_len, dtype=jnp.float32)
            diff = n[:, None] - n[None, :]
            mask = diff >= 0
            D = jnp.where(mask, gamma ** jnp.where(mask, diff, 0.0), 0.0)
            return D

        def _reference_tuple_inner(x, W_Q, W_K, W_V):
            S = x.shape[1]
            D = get_D(GAMMA, S)
            Q = xpos_rope(x @ W_Q, downscale=False)
            K = xpos_rope(x @ W_K, downscale=True)
            V = x @ W_V
            ret = jnp.einsum('bnd,bmd->bnm', Q, K) * D[None, :, :]
            out = jnp.einsum('bnm,bmv->bnv', ret, V)
            return (out, ret)
        return _reference_tuple_inner(x, W_Q, W_K, W_V)[0]

    def _L0_ffn_ref(x, Wg, bg, W1, b1, W2, b2):
        import jax, jax.numpy as jnp
        import numpy as np
        B, S, D, E, H, K = (4, 1024, 64, 8, 128, 2)
        Bv, Sv, Dv = x.shape
        gate_scores = x @ Wg + bg
        _, idx = jax.lax.top_k(gate_scores, K)
        mask = jax.nn.one_hot(idx, E, dtype=x.dtype).sum(axis=-2)
        xf = x.reshape(-1, Dv)
        mf = mask.reshape(-1, E)
        h = jax.nn.gelu(jnp.einsum('td,edh->teh', xf, W1) + b1[None], approximate=False)
        y = jnp.einsum('teh,ehd->ted', h, W2) + b2[None]
        out = jnp.einsum('ted,te->td', y, mf)
        return out.reshape(Bv, Sv, Dv)
    h = _L0_tok_ref(x, L0_tok_conv1_w, L0_tok_conv1_b, L0_tok_bn_gamma, L0_tok_bn_beta, L0_tok_bn_mean, L0_tok_bn_var, L0_tok_conv2_w, L0_tok_conv2_b)
    h = jnp.concatenate([jnp.broadcast_to(cls_tok, (h.shape[0], 1, h.shape[2])), h], axis=1)
    h = h + _L0_attn_ref(_layernorm(h, axis=-1), L0_attn_W_Q, L0_attn_W_K, L0_attn_W_V)
    h = h + _L0_ffn_ref(_layernorm(h, axis=-1), L0_ffn_Wg, L0_ffn_bg, L0_ffn_W1, L0_ffn_b1, L0_ffn_W2, L0_ffn_b2)
    return h

_drawn_inputs = setup_inputs


def setup_inputs(seed=0):
    import zlib

    import numpy as np

    out = dict(_drawn_inputs(seed))
    spreads = {'L0_tok_conv1_b': (0.0, 0.1),
     'L0_tok_bn_gamma': (1.0, 0.2),
     'L0_tok_bn_beta': (0.0, 0.1),
     'L0_tok_bn_mean': (0.0, 0.1),
     'L0_tok_bn_var': (1.0, 0.2),
     'L0_tok_conv2_b': (0.0, 0.1),
     'L0_ffn_bg': (0.0, 0.1),
     'L0_ffn_b1': (0.0, 0.8),
     'L0_ffn_b2': (0.0, 0.1)}
    factors = {'cls_tok': 200.0, 'L0_ffn_W1': 4.534, 'L0_ffn_W2': 3.824}
    for name, (base, spread) in spreads.items():
        noise = np.random.default_rng([zlib.crc32(name.encode()), seed]).standard_normal(out[name].shape)
        drawn = base * np.exp(spread * noise) if base else spread * noise
        out[name] = jnp.asarray(drawn.astype(out[name].dtype))
    for name, factor in factors.items():
        out[name] = (out[name] * factor).astype(out[name].dtype)
    return out
```

```python
import concourse.bass as bass
from concourse import mybir
from contextlib import ExitStack

F32 = mybir.dt.float32
F32R = mybir.dt.float32r
ACT = mybir.ActivationFunctionType
ALU = mybir.AluOpType
AX = mybir.AxisListType

P = 128
D = 64
NB = 4
IMG = 64
HW = IMG * IMG
SEQ = HW + 1
C = 128
CPT = 4
NT = CPT * C
TURNS = HW // NT
ROWS = NT // IMG
E = 8
HID = 128
TAPS = 9
CR = 16
GAMMA = 0.96875
LN_EPS = 1e-5
BN_EPS = 1e-5
OFF = -(2.0 ** 100)
VEC_TAPS = (4, 0, 1, 2)
POOL_TAPS = (3, 5, 6, 7, 8)
TAP_ORDER = VEC_TAPS + POOL_TAPS


def build(nc, x, cls, conv1, bnp, conv2, colmask, sel, wqkv, w1hi, w1lo, w2, b2, wg, bg,
          tabq, tabk, tabc, causal, order, out):
    ctx = ExitStack()
    with ctx:
        def sb(name, shape, dt=F32):
            return ctx.enter_context(nc.sbuf_tensor(name, shape, dt))

        def sem(name):
            return ctx.enter_context(nc.semaphore(name))

        mixed = nc.dram_tensor("mixed", [NB, IMG, IMG, IMG], F32, kind="Internal").ap()

        ident = sb("ident", [P, P])
        selt = sb("selt", [P, 8])
        conv1_t = sb("conv1_t", [P, 96])
        bn_t = sb("bn_t", [96, 5])
        bn_s = sb("bn_s", [96, 4])
        neghalf = sb("neghalf", [P, 8])
        c2 = sb("c2", [P, 4, TAPS])
        mask_cols = sb("mask_cols", [P, P])
        conv2_t = sb("conv2_t", [P, TAPS, P], F32R)
        qkv_raw = sb("qkv_raw", [P, 320])
        qkv_hi = sb("qkv_hi", [P, 320], F32R)
        qkv_lo = sb("qkv_lo", [P, 320], F32R)
        w1_hi = sb("w1_hi", [P, E * HID], F32R)
        w1_lo = sb("w1_lo", [P, E * HID], F32R)
        w2_t = sb("w2_t", [P, E * D])
        b2_t = sb("b2_t", [P, P], F32R)
        wg_raw = sb("wg_raw", [P, E])
        wg_t = sb("wg_t", [P, 2 * E], F32R)
        bg_t = sb("bg_t", [P, E])
        order_t = sb("order_t", [P, E])
        causal_t = sb("causal_t", [P, C])
        tabc_t = sb("tabc_t", [P, 2 * C])
        tabq_t = sb("tabq_t", [P, HW])
        tabk_t = sb("tabk_t", [P, HW])

        ximg = [sb(f"ximg{p}", [P, (IMG + 2) * IMG]) for p in range(2)]
        y_st = sb("y_st", [P, NT], F32R)
        y_f = sb("y_f", [64, NT])
        prod = sb("prod", [P, len(POOL_TAPS) + 1, NT])
        acc = [sb(f"acc{i}", [P, NT]) for i in range(2)]

        h1 = sb("h1", [P, 8, D])
        xm = sb("xm", [P, 8, D])
        sq = sb("sq", [P, 8, D])
        zf = sq
        st = sb("st", [P, 6, 8])
        ztok = sb("ztok", [P, 8, 2 * D], F32R)
        z_t = sb("z_t", [P, 2 * NT], F32R)
        q_t = sb("q_t", [P, 2 * NT])
        km = sb("km", [P, 8, 2 * D])
        kd = sb("kd", [P, 8, 2 * D])
        v_tok = sb("v_tok", [P, 8, D])
        k_t = sb("k_t", [P, 2 * NT])
        prob = sb("prob", [P, 2 * NT])
        u_cls = sb("u_cls", [P, D])
        u_car = sb("u_car", [P, 2, D])
        u_in = sb("u_in", [P, CPT, 2, D])
        h2n = sb("h2n", [P, 8, D])
        h2 = sb("h2", [P, TURNS + 1, 8, D])

        ftok = sb("ftok", [P, 8, 3 * D], F32R)
        g_t = sb("g_t", [P, 2 * NT], F32R)
        f1_t = sb("f1_t", [P, 2 * NT], F32R)
        f2_t = sb("f2_t", [P, 2 * NT], F32R)
        gs = sb("gs", [P, 6, 8, E])
        gm = sb("gm", [P, 4, 8])
        hid = sb("hid", [P, 8, NT])
        w1_raw = hid[:, 0:2, :].rearrange("p a b -> p (a b)")
        w1_tmp = hid[:, 2:4, :].rearrange("p a b -> p (a b)")
        b2_raw, b2_tmp = hid[:, 4, 0:P], hid[:, 5, 0:2 * P]
        y_sb = sb("y_sb", [P, 2, NT])
        o_t = sb("o_t", [P, 8, D])

        zb = [ctx.enter_context(nc.psum_tensor(f"zb{i}", [P, NT], F32)) for i in range(2)]
        yb = [ctx.enter_context(nc.psum_tensor(f"yb{i}", [P, NT], F32)) for i in range(2)]
        mb = [ctx.enter_context(nc.psum_tensor(f"mb{i}", [P, NT], F32)) for i in range(4)]

        ld_x = [sem(f"ld_x{p}") for p in range(2)]
        ld_tok, ld_att, ld_ffn, ld_tabs = sem("ld_tok"), sem("ld_att"), sem("ld_ffn"), sem("ld_tabs")
        ld_h1 = sem("ld_h1")
        stored_tok = [sem(f"stored_tok{i}") for i in range(2)]
        stored_out = sem("stored_out")
        id_steps, pool_steps, vec_steps = sem("id_steps"), sem("pool_steps"), sem("vec_steps")
        guards, bn_scale, bn_bias, conv2_ready = sem("guards"), sem("bn_scale"), sem("bn_bias"), sem("conv2_ready")
        att_w, ffn_w = sem("att_w"), sem("ffn_w")
        conv1_done, relu_done, ylo_done = sem("conv1_done"), sem("relu_done"), sem("ylo_done")
        tap_bc, tap_mul, vec_sum, pool_sum = sem("tap_bc"), sem("tap_mul"), sem("vec_sum"), sem("pool_sum")
        centred, squared, sumsq, rstd, normed = sem("centred"), sem("squared"), sem("sumsq"), sem("rstd"), sem("normed")
        zt_ps, zt_sb, q_ps, q_sb, kv_ps = sem("zt_ps"), sem("zt_sb"), sem("q_ps"), sem("q_sb"), sem("kv_ps")
        k_mul, k_rot, v_sb, kt_ps, kt_sb = sem("k_mul"), sem("k_rot"), sem("v_sb"), sem("kt_ps"), sem("kt_sb")
        sc_ps, prob_sb, du_ps, u_done = sem("sc_ps"), sem("prob_sb"), sem("du_ps"), sem("u_done")
        at_ps, h2_done, h2_kept = sem("at_ps"), sem("h2_done"), sem("h2_kept")
        gt_ps, gt_sb, gate_ps, gated = sem("gt_ps"), sem("gt_sb"), sem("gate_ps"), sem("gated")
        f2_ps, f2_sb, f1_sb = sem("f2_ps"), sem("f2_sb"), sem("f1_sb")
        hid_ps, hid_sb, y_ps, y_ev, yt_ps, o_done = (
            sem("hid_ps"), sem("hid_sb"), sem("y_ps"), sem("y_ev"), sem("yt_ps"), sem("o_done"))

        def upto(t, per, j, first):
            if isinstance(t, int) and t == 0:
                return j
            return (t - 1) * per + (first + j)

        def batches(t):
            return 1 if isinstance(t, int) and t == 0 else 2

        def chunks(t):
            return 1 if isinstance(t, int) and t == 0 else CPT

        def w_range(k):
            dj = k % 3 - 1
            return max(0, -dj), IMG - max(0, dj)

        def h2_of(t, pair1):
            if isinstance(t, int):
                g = TURNS if t == 0 else (t - 1) % TURNS
            else:
                g = t - 9 if pair1 else t - 1
            return h2[:, bass.ds(g, 1)]

        block = ctx.enter_context(nc.Block())

        def all_turns(eng, body):
            body(0, 0, 9)
            with eng.Fori(1, 7) as f:
                body(f, f, f + 9)
            body(7, 7, None)
            body(8, 0, None)
            with eng.Fori(9, 15) as f:
                body(f, f - 8, None)
            body(15, 7, None)
            body(16, None, None)

        @block.sync
        def _(sp):
            sp.dma_start(conv1_t[:, :], conv1).then_inc(ld_tok, 16)
            sp.dma_start(bn_t[:, :], bnp).then_inc(ld_tok, 16)
            sp.dma_start(c2[:, 0, :], conv2).then_inc(ld_tok, 16)
            sp.dma_start(mask_cols[:, :], colmask).then_inc(ld_tok, 16)
            sp.dma_start(selt[:, :], sel).then_inc(ld_tok, 16)
            sp.dma_start(ximg[0][:, IMG:IMG + HW], x[0]).then_inc(ld_x[0], 16)
            for dst, src in ((qkv_raw, wqkv), (causal_t, causal), (tabc_t, tabc)):
                sp.dma_start(dst[:, :], src).then_inc(ld_att, 16)
            for dst, src in ((w1_raw, w1hi), (w1_tmp, w1lo), (w2_t, w2), (b2_raw, b2), (wg_raw, wg),
                             (bg_t, bg), (order_t, order)):
                sp.dma_start(dst[:, :], src).then_inc(ld_ffn, 16)
            sp.dma_start(h1[:, 0, :], cls.to_broadcast([P, D])).then_inc(ld_h1, 16)
            sp.dma_start(ximg[1][:, IMG:IMG + HW], x[1]).then_inc(ld_x[1], 16)
            sp.dma_start(tabq_t[:, :], tabq).then_inc(ld_tabs, 16)
            sp.dma_start(tabk_t[:, :], tabk).then_inc(ld_tabs, 16)

            def store_tok(q, slot, pair, g):
                sp.wait_ge(pool_sum, (q + 1) * len(POOL_TAPS))
                for b in range(2):
                    sp.dma_start(mixed[2 * pair + b, :, bass.ds(g * ROWS, ROWS), :],
                                 acc[slot][64 * b:64 * b + 64, :].rearrange("c (r w) -> c r w", w=IMG))\
                      .then_inc(stored_tok[slot], 16)

            def load_h1(t, pair, g):
                sp.wait_ge(h2_done, t)
                for b in range(2):
                    src = mixed[2 * pair + b].rearrange("c h w -> (c h) w")[bass.ds(g * NT, NT), :]
                    sp.dma_start(h1[:, CPT * b:CPT * b + CPT, :], src.rearrange("(c p) w -> p c w", p=C))\
                      .then_inc(ld_h1, 16)

            with sp.Fori(0, TURNS // 2) as i:
                store_tok(2 * i, 0, 0, 2 * i)
                store_tok(2 * i + 1, 1, 0, 2 * i + 1)
            store_tok(8, 0, 1, 0)
            sp.wait_ge(stored_tok[0], 32 * 5)
            sp.wait_ge(stored_tok[1], 32 * 4)
            load_h1(1, 0, 0)

            def body(f, a, tile):
                if tile is not None:
                    store_tok(tile, 0, 1, tile - 8)
                if isinstance(f, int) and f == 7:
                    sp.wait_ge(stored_tok[0], 32 * 12)
                    load_h1(9, 1, 0)
                elif a is not None and not (isinstance(f, int) and f == 15):
                    pair = 0 if tile is not None else 1
                    load_h1(f + 2, pair, a + 1)
                nb = batches(f)
                for b in range(nb):
                    sp.wait_ge(o_done, upto(f, 2, b + 1, 1))
                    if isinstance(f, int) and f == 0:
                        sp.dma_start(out[:, 0, :], o_t[0:NB, 0, :]).then_inc(stored_out, 16)
                        continue
                    second = not isinstance(f, int) and tile is None or isinstance(f, int) and f > 8
                    g = f - 9 if second else f - 1
                    dst = out[2 * second + b, bass.ds(g * NT + 1, NT), :]
                    sp.dma_start(dst.rearrange("(c p) w -> p c w", p=C), o_t[:, CPT * b:CPT * b + CPT, :])\
                      .then_inc(stored_out, 16)

            all_turns(sp, body)
            sp.wait_ge(stored_out, 16 + 32 * 16)

        @block.gpsimd
        def _(pool):
            for p in range(2):
                pool.memset(ximg[p][:, 0:IMG], 0.0).then_inc(guards, 1)
                pool.memset(ximg[p][:, IMG + HW:], 0.0).then_inc(guards, 1)
            pool.memset(ident[:, :], 0.0).then_inc(id_steps, 1)
            pool.memset(ftok[:, :, 128:192].bitcast(F32), 0.0).then_inc(id_steps, 1)
            pool.memset(neghalf[:, :], -0.5).then_inc(id_steps, 1)
            pool.wait_ge(id_steps, 3)
            pool.memset(ftok[:, :, 136:138].bitcast(F32), 1.0).then_inc(guards, 1)
            pool.affine_select(out=ident[:, :], in_=ident[:, :], compare_op=ALU.not_equal, fill=1.0,
                               base=0, pattern=[[-1, P]], channel_multiplier=1).then_inc(guards, 1)
            pool.wait_ge(ld_tok, 80)
            pool.tensor_scalar(bn_s[:, 0:1], bn_t[:, 4:5], 1.0, BN_EPS, ALU.mult, ALU.add).then_inc(pool_steps, 1)
            pool.wait_ge(pool_steps, 1)
            pool.tensor_tensor(bn_s[:, 1:2], bn_s[:, 0:1], neghalf[0:96, 0:1], ALU.pow).then_inc(bn_scale, 1)

            def tile(q, slot, lo_j=0, hi_j=len(POOL_TAPS)):
                for j, k in list(enumerate(POOL_TAPS))[lo_j:hi_j]:
                    pool.wait_ge(tap_mul, q * TAPS + TAP_ORDER.index(k) + 1)
                    if j == 0:
                        pool.wait_ge(vec_sum, q + 1)
                    else:
                        pool.wait_ge(pool_sum, q * len(POOL_TAPS) + j)
                    lo, hi = w_range(k)
                    a = acc[slot][:, :].rearrange("p (r w) -> p r w", w=IMG)[:, :, lo:hi]
                    pr = prod[:, j, :].rearrange("p (r w) -> p r w", w=IMG)[:, :, lo:hi]
                    pool.tensor_tensor(a, a, pr, ALU.add).then_inc(pool_sum, 1)

            def rsqrt(n, width):
                pool.wait_ge(sumsq, n + 1)
                pool.tensor_tensor(st[:, 4, 0:width], st[:, 3, 0:width], neghalf[:, 0:width], ALU.pow)\
                    .then_inc(rstd, 1)

            with pool.Fori(0, TURNS // 2) as i:
                tile(2 * i, 0)
                tile(2 * i + 1, 1)
            tile(8, 0)
            rsqrt(0, 1)
            rsqrt(1, 1)
            rsqrt(2, 8)

            def body(f, a, q):
                if q is not None:
                    tile(q, 0, 0, 1)
                if a is not None:
                    rsqrt(2 * f + 3, 8)
                if q is not None:
                    tile(q, 0, 1)
                if a is not None:
                    if not (isinstance(f, int) and f == 15):
                        rsqrt(2 * f + 4, 8)

            all_turns(pool, body)

        @block.scalar
        def _(act):
            def relu(q, bank):
                act.wait_ge(conv1_done, q + 1)
                act.activation(y_st[0:96, :], bank[0:96, :], ACT.Relu, bias=bn_s[:, 2:3], scale=bn_s[:, 1:2])\
                   .then_inc(relu_done, 1)
                act.activation(y_f[32:64, :], bank[32:64, :], ACT.Relu, bias=bn_s[32:64, 2:3],
                               scale=bn_s[32:64, 1:2]).then_inc(relu_done, 1)

            def square(n, width):
                act.wait_ge(centred, n + 1)
                act.activation(sq[:, 0:width, :], xm[:, 0:width, :], ACT.Square).then_inc(squared, 1)

            def keep_h2(t, pair1):
                width = 8 if batches(t) == 2 else 1
                act.wait_ge(h2_done, t + 1)
                act.activation(h2_of(t, pair1)[:, :, 0:width, :].rearrange("p a c d -> p (a c) d"),
                               h2n[:, 0:width, :], ACT.Copy).then_inc(h2_kept, 1)

            def z_out(t):
                for b in range(batches(t)):
                    n = chunks(t) * C
                    act.wait_ge(zt_ps, upto(t, 2, b + 1, 1))
                    act.activation(z_t[:, b * NT:b * NT + n], mb[b][:, 0:n], ACT.Copy).then_inc(zt_sb, 1)

            def v_out(t, u):
                n = min(2, chunks(t))
                act.wait_ge(k_mul, upto(t, 4, u + 1, 1))
                kv = mb[u % 2][:, 0:n * 192].rearrange("p (c k) -> p c k", k=192)
                act.activation(v_tok[:, 2 * u:2 * u + n, :], kv[:, :, 128:192], ACT.Copy).then_inc(v_sb, 1)

            def kt_out(t, b):
                n = chunks(t) * C
                act.wait_ge(kt_ps, upto(t, 2, b + 1, 1))
                act.activation(k_t[:, b * NT:b * NT + n], mb[b][:, 0:n], ACT.Copy).then_inc(kt_sb, 1)

            def gt_out(t, b):
                n = chunks(t) * C
                act.wait_ge(gt_ps, upto(t, 2, b + 1, 1))
                if not (isinstance(t, int) and t == 0):
                    act.wait_ge(f1_sb, t)
                act.activation(g_t[:, b * NT:b * NT + n], mb[b][:, 0:n], ACT.Copy).then_inc(gt_sb, 1)

            def f2_out(t, b):
                n = chunks(t) * C
                act.wait_ge(f2_ps, upto(t, 2, b + 1, 1))
                act.activation(f2_t[:, b * NT:b * NT + n], mb[1 - b][:, 0:n], ACT.Copy).then_inc(f2_sb, 1)

            def gelu(f, s):
                n = chunks(f) * C
                act.wait_ge(hid_ps, upto(f, 16, s + 1, 8))
                act.activation(hid[:, s % 8, 0:n], zb[s % 2][:, 0:n], ACT.Gelu).then_inc(hid_sb, 1)

            def y_out(f, b):
                n = chunks(f) * C
                act.wait_ge(y_ps, upto(f, 2, b + 1, 1))
                act.activation(y_sb[:, b, 0:n], yb[b][:, 0:n], ACT.Copy).then_inc(y_ev, 1)

            act.wait_ge(bn_bias, 1)
            with act.Fori(0, TURNS // 2) as i:
                relu(2 * i, yb[0])
                relu(2 * i + 1, yb[0])
            relu(8, yb[0])
            square(0, 1)
            z_out(0)
            v_out(0, 0)
            kt_out(0, 0)
            square(1, 1)
            keep_h2(0, False)
            gt_out(0, 0)
            f2_out(0, 0)
            square(2, 8)

            def body(f, a, q):
                nb = batches(f)

                def slots(lo, hi):
                    for s in range(lo, hi):
                        if s % 2 < nb:
                            gelu(f, s if nb == 2 else s // 2)

                t = f + 1
                slots(0, 1)
                if q is not None:
                    relu(q, mb[2])
                slots(1, 3)
                if a is not None:
                    z_out(t)
                slots(3, 5)
                if a is not None:
                    v_out(t, 0)
                    v_out(t, 1)
                slots(5, 6)
                if a is not None:
                    v_out(t, 2)
                    v_out(t, 3)
                slots(6, 8)
                if a is not None:
                    kt_out(t, 0)
                    kt_out(t, 1)
                slots(8, 12)
                if a is not None:
                    square(2 * f + 3, 8)
                    keep_h2(t, q is None)
                slots(12, 14)
                if a is not None:
                    gt_out(t, 0)
                    gt_out(t, 1)
                slots(14, 16)
                for b in range(nb):
                    y_out(f, b)
                if a is not None:
                    for b in range(2):
                        f2_out(t, b)
                    if not (isinstance(f, int) and f == 15):
                        square(2 * f + 4, 8)

            all_turns(act, body)

        @block.tensor
        def _(pe):
            def conv1_mm(q, pair, g, bank, free=None):
                if free is not None:
                    pe.wait_ge(*free)
                pe.matmul(bank[0:96, :], conv1_t[:, :], ximg[pair][:, bass.ds(g * NT + IMG, NT)],
                          start=True, stop=True).then_inc(conv1_done, 1)

            def tap_mm(q, j, bank, before):
                if j == 0:
                    pe.wait_ge(ylo_done, q + 1)
                    pe.wait_ge(relu_done, 2 * q + 2)
                if before is not None:
                    pe.wait_ge(tap_mul, before)
                pe.matmul(bank[:, :], conv2_t[:, TAP_ORDER[j], :], y_st[:, :], start=True, stop=True)\
                  .then_inc(tap_bc, 1)

            def z_mm(t):
                n = chunks(t)
                pe.wait_ge(normed, 2 * t + 1)
                for b in range(batches(t)):
                    if not (isinstance(t, int) and t == 0):
                        if isinstance(t, int) and t == 1:
                            pe.wait_ge(f2_sb, 1)
                        else:
                            pe.wait_ge(f2_sb, upto(t - 1, 2, 2, 1))
                    for c in range(n):
                        k = CPT * b + c
                        last = pe.transpose(mb[b][:, c * C:c * C + C], ztok[:, k, :].bitcast(F32), ident[:, :])
                    last.then_inc(zt_ps, 1)

            def q_mm(t):
                n = chunks(t) * C
                for b in range(batches(t)):
                    pe.wait_ge(zt_sb, upto(t, 2, b + 1, 1))
                    z = z_t[:, b * NT:b * NT + n]
                    pe.matmul(mb[b][:, 0:n], qkv_hi[:, 0:128], z, start=True, stop=False)
                    pe.matmul(mb[b][:, 0:n], qkv_lo[:, 0:128], z, start=False, stop=True).then_inc(q_ps, 1)

            def kv_mm(t, u):
                if u < 2:
                    pe.wait_ge(q_sb, upto(t, 2, u + 1, 1))
                else:
                    pe.wait_ge(v_sb, upto(t, 4, u - 1, 1))
                for c in range(min(2, chunks(t))):
                    k = 2 * u + c
                    z = z_t[:, k * C:k * C + C]
                    o = mb[u % 2][:, c * 192:c * 192 + 192]
                    pe.matmul(o, z, qkv_hi[:, 128:320], start=True, stop=False)
                    last = pe.matmul(o, z, qkv_lo[:, 128:320], start=False, stop=True)
                last.then_inc(kv_ps, 1)

            def kt_mm(t, b):
                pe.wait_ge(k_rot, upto(t, 2, b + 1, 1))
                pe.wait_ge(v_sb, upto(t, 4, 3 + b, 1) if batches(t) == 2 else 1)
                for c in range(chunks(t)):
                    k = CPT * b + c
                    last = pe.transpose(mb[b][:, c * C:c * C + C], kd[:, k, :], ident[:, :])
                last.then_inc(kt_ps, 1)

            def score_mm(t, b):
                pe.wait_ge(kt_sb, upto(t, 2, b + 1, 1))
                for c in range(chunks(t)):
                    k = CPT * b + c
                    last = pe.matmul(mb[b][:, c * C:c * C + C], k_t[:, k * C:k * C + C],
                                     q_t[:, k * C:k * C + C], start=True, stop=True)
                last.then_inc(sc_ps, 1)

            def du_mm(t):
                pe.wait_ge(prob_sb, upto(t, 2, 1, 1))
                if isinstance(t, int) and t == 0:
                    pe.matmul(mb[0][:, 0:D], kd[0:1, 0, :], v_tok[0:1, 0, :], start=True, stop=True)\
                      .then_inc(du_ps, 1)
                    return
                for k in range(8):
                    last = pe.matmul(mb[0][:, k * D:k * D + D], kd[:, k, :], v_tok[:, k, :], start=True, stop=True)
                last.then_inc(du_ps, 1)

            def at_mm(t):
                cls_turn = isinstance(t, int) and t == 0
                pe.wait_ge(prob_sb, upto(t, 2, batches(t), 1))
                if not cls_turn:
                    pe.wait_ge(u_done, t + 1)
                for b in range(batches(t)):
                    for c in range(chunks(t)):
                        k = CPT * b + c
                        o = mb[1][:, k * D:k * D + D]
                        last = pe.matmul(o, prob[:, k * C:k * C + C], v_tok[:, k, :], start=True, stop=cls_turn)
                        if not cls_turn:
                            u = u_car[:, b, :] if c == 0 else u_in[:, c, b, :]
                            last = pe.matmul(o, q_t[:, k * C:k * C + C], u, start=False, stop=True)
                last.then_inc(at_ps, 1)

            def gt_mm(t):
                pe.wait_ge(normed, 2 * t + 2)
                for b in range(batches(t)):
                    for c in range(chunks(t)):
                        k = CPT * b + c
                        last = pe.transpose(mb[b][:, c * C:c * C + C], ftok[:, k, 0:128].bitcast(F32), ident[:, :])
                    last.then_inc(gt_ps, 1)

            def gate_mm(t):
                pe.wait_ge(gt_sb, upto(t, 2, batches(t), 1))
                for b in range(batches(t)):
                    for c in range(chunks(t)):
                        k = CPT * b + c
                        last = pe.matmul(mb[0][:, k * 16:k * 16 + 16], g_t[:, k * C:k * C + C], wg_t[:, :],
                                         start=True, stop=True)
                last.then_inc(gate_ps, 1)

            def f2_mm(t):
                pe.wait_ge(gated, t + 1)
                for b in range(batches(t)):
                    for c in range(chunks(t)):
                        k = CPT * b + c
                        last = pe.transpose(mb[1 - b][:, c * C:c * C + C], ftok[:, k, 64:192].bitcast(F32),
                                            ident[:, :])
                    last.then_inc(f2_ps, 1)

            def w1_mm(f, s):
                nb, n = batches(f), chunks(f) * C
                e, b = s // nb, s % nb
                if e == 0:
                    pe.wait_ge(f2_sb, upto(f, 2, b + 1, 1))
                    pe.wait_ge(f1_sb, f + 1)
                    if not (isinstance(f, int) and f == 0):
                        if isinstance(f, int) and f == 1:
                            pe.wait_ge(y_ev, 1)
                        else:
                            pe.wait_ge(y_ev, upto(f - 1, 2, 2, 1))
                    pe.matmul(yb[b][:, 0:n], b2_t[:, :], f2_t[:, b * NT:b * NT + n], start=True, stop=False)
                if isinstance(f, int) and f == 0:
                    if s >= 2:
                        pe.wait_ge(hid_sb, s - 1)
                else:
                    pe.wait_ge(hid_sb, upto(f, 16, s - 1, 8))
                w = slice(e * HID, e * HID + HID)
                pe.matmul(zb[s % 2][:, 0:n], w1_hi[:, w], f1_t[:, b * NT:b * NT + n], start=True, stop=False)
                pe.matmul(zb[s % 2][:, 0:n], w1_lo[:, w], f2_t[:, b * NT:b * NT + n], start=False, stop=True)\
                  .then_inc(hid_ps, 1)

            def w2_mm(f, j, b):
                nb, n = batches(f), chunks(f) * C
                s0, s1 = 2 * j * nb + b, (2 * j + 1) * nb + b
                pe.wait_ge(hid_sb, upto(f, 16, s1 + 1, 8))
                pe.matmul(yb[b][0:64, 0:n], w2_t[:, 2 * j * D:2 * j * D + D], hid[:, s0 % 8, 0:n],
                          start=False, stop=j == 3)
                last = pe.matmul(yb[b][64:128, 0:n], w2_t[:, (2 * j + 1) * D:(2 * j + 2) * D],
                                 hid[:, s1 % 8, 0:n], start=False, stop=j == 3)
                if j == 3:
                    last.then_inc(y_ps, 1)

            def yt_mm(f, b, tap_before):
                if tap_before is not None:
                    pe.wait_ge(tap_mul, tap_before)
                else:
                    pe.wait_ge(o_done, upto(f, 2, 0, 1))
                pe.wait_ge(y_ev, upto(f, 2, b + 1, 1))
                for c in range(chunks(f)):
                    last = pe.transpose(mb[2 + b][:, c * C:c * C + C], y_sb[:, b, c * C:c * C + C], ident[:, :])
                last.then_inc(yt_ps, 1)

            pe.wait_ge(ld_tok, 80)
            pe.wait_ge(ld_x[0], 16)
            pe.wait_ge(guards, 7)
            pe.wait_ge(conv2_ready, 1)
            ring = [zb[0], zb[1], yb[1], mb[0], mb[1], mb[2], mb[3]]

            def first_tile(q, pair, g, checked):
                conv1_mm(q, pair, g, yb[0])
                for j in range(TAPS):
                    if j >= 7:
                        before = q * TAPS + j - 6
                    elif checked:
                        before = (q - 1) * TAPS + (j + 8 if j < 2 else j + 1)
                    else:
                        before = None
                    tap_mm(q, j, ring[j % 7], before)

            first_tile(0, 0, 0, False)
            pe.wait_ge(relu_done, 2)
            first_tile(1, 0, 1, True)
            with pe.Fori(1, TURNS // 2) as i:
                for j in range(2):
                    pe.wait_ge(relu_done, 4 * i + 2 * j)
                    first_tile(2 * i + j, 0, 2 * i + j, True)
            pe.wait_ge(ld_x[1], 16)
            pe.wait_ge(relu_done, 16)
            first_tile(8, 1, 0, True)

            pe.wait_ge(tap_mul, 9 * TAPS)
            pe.wait_ge(att_w, 1)
            z_mm(0)
            q_mm(0)
            kv_mm(0, 0)
            kt_mm(0, 0)
            score_mm(0, 0)
            du_mm(0)
            at_mm(0)
            pe.wait_ge(u_done, 1)
            gt_mm(0)
            pe.wait_ge(ffn_w, 1)
            gate_mm(0)
            f2_mm(0)

            def body(f, a, q):
                nb, t = batches(f), f + 1

                def slot(s):
                    if s % 2 < nb:
                        w1_mm(f, s if nb == 2 else s // 2)
                    if s >= 4 and s % 4 < nb:
                        w2_mm(f, s // 4 - 1, s % 4)

                def tap(j):
                    if q is not None:
                        before = None if j < 2 else q * TAPS + j - 1
                        tap_mm(q, j, mb[3 - j % 2], before)

                slot(0)
                if q is not None:
                    if not (isinstance(f, int) and f == 0):
                        pe.wait_ge(o_done, upto(f, 2, 0, 1))
                    conv1_mm(q, 1, q - 8, mb[2])
                slot(1)
                slot(2)
                if a is not None:
                    z_mm(t)
                slot(3)
                if a is not None:
                    q_mm(t)
                slot(4)
                if a is not None:
                    kv_mm(t, 0)
                    kv_mm(t, 1)
                slot(5)
                tap(0)
                tap(1)
                if a is not None:
                    kv_mm(t, 2)
                    kv_mm(t, 3)
                slot(6)
                tap(2)
                slot(7)
                if a is not None:
                    kt_mm(t, 0)
                    kt_mm(t, 1)
                slot(8)
                if a is not None:
                    score_mm(t, 0)
                    score_mm(t, 1)
                tap(3)
                slot(9)
                if a is not None:
                    du_mm(t)
                slot(10)
                if a is not None:
                    at_mm(t)
                tap(4)
                slot(11)
                tap(5)
                slot(12)
                tap(6)
                slot(13)
                if a is not None:
                    gt_mm(t)
                tap(7)
                slot(14)
                if a is not None:
                    gate_mm(t)
                tap(8)
                slot(15)
                for b in range(nb):
                    w2_mm(f, 3, b)
                yt_mm(f, 0, None if q is None else q * TAPS + 9)
                if a is not None:
                    f2_mm(t)
                if nb == 2:
                    yt_mm(f, 1, None if q is None else q * TAPS + 9)

            all_turns(pe, body)

        @block.vector
        def _(dve):
            made = [0, None, 0]

            def step(ins):
                ins.then_inc(vec_steps, 1)
                made[2] += 1

            def settled():
                if made[1] is None:
                    dve.wait_ge(vec_steps, made[0] + made[2])
                else:
                    i, per = made[1]
                    dve.wait_ge(vec_steps, i * per + (made[0] + made[2]))

            def flush():
                made[0] += made[2]
                made[2] = 0

            step(dve.memset(y_st[96:128, :].bitcast(F32), 0.0))
            settled()
            dve.memset(y_st[96:98, :].bitcast(F32), 1.0).then_inc(guards, 1)
            dve.wait_ge(ld_tok, 80)
            w = c2[:, 0, :]
            hi, lo = c2[:, 1, :].bitcast(F32R), c2[:, 2, :]
            step(dve.tensor_copy(hi, w))
            dve.wait_ge(bn_scale, 1)
            step(dve.tensor_tensor(bn_s[:, 1:2], bn_s[:, 1:2], bn_t[:, 1:2], ALU.mult))
            step(dve.tensor_tensor(bn_s[:, 3:4], bn_t[:, 0:1], bn_t[:, 3:4], ALU.subtract))
            settled()
            step(dve.tensor_tensor(lo, w, hi.bitcast(F32), ALU.subtract))
            dve.scalar_tensor_tensor(bn_s[:, 2:3], bn_s[:, 3:4], bn_s[:, 1:2], bn_t[:, 2:3], ALU.mult, ALU.add)\
               .then_inc(bn_bias, 1)
            settled()
            step(dve.tensor_scalar(lo, lo, selt[:, 1:2], None, ALU.mult))
            settled()
            step(dve.scalar_tensor_tensor(c2[:, 3, :], hi.bitcast(F32), selt[:, 0:1], lo, ALU.mult, ALU.add))
            settled()
            dve.tensor_tensor(conv2_t[:, :, :], c2[:, 3, :].unsqueeze(2).broadcast_to([P, TAPS, P]),
                              mask_cols[:, :].unsqueeze(1).broadcast_to([P, TAPS, P]), ALU.mult)\
               .then_inc(conv2_ready, 1)

            def y_low(q):
                dve.wait_ge(relu_done, 2 * q + 2)
                dve.tensor_tensor(y_st[32:64, :], y_f[32:64, :], y_st[32:64, :].bitcast(F32), ALU.subtract)\
                   .then_inc(ylo_done, 1)

            def tap(q, j, pair, g, slot, bank, stores):
                k = TAP_ORDER[j]
                di = k // 3 - 1
                lo_, hi_ = w_range(k)
                dj = k % 3 - 1
                img = ximg[pair][:, bass.ds((g * ROWS + 1 + di) * IMG, ROWS * IMG)]\
                    .rearrange("p (r w) -> p r w", w=IMG)[:, :, lo_ + dj:hi_ + dj]
                wt = bank[:, :].rearrange("p (r w) -> p r w", w=IMG)[:, :, lo_:hi_]
                dst = acc[slot] if j == 0 else prod[:, POOL_TAPS.index(k) if k in POOL_TAPS else len(POOL_TAPS)]
                view = dst[:, :].rearrange("p (r w) -> p r w", w=IMG)[:, :, lo_:hi_]
                if j == 0 and stores is not None:
                    dve.wait_ge(stored_tok[slot], stores)
                if k in VEC_TAPS[2:]:
                    settled()
                dve.wait_ge(tap_bc, q * TAPS + j + 1)
                dve.tensor_tensor(view, wt, img, ALU.mult).then_inc(tap_mul, 1)
                if k in VEC_TAPS[1:]:
                    dve.wait_ge(tap_mul, q * TAPS + j + 1)
                    settled()
                    a = acc[slot][:, :].rearrange("p (r w) -> p r w", w=IMG)[:, :, lo_:hi_]
                    add = dve.tensor_tensor(a, a, view, ALU.add)
                    if k == VEC_TAPS[-1]:
                        add.then_inc(vec_sum, 1)
                    else:
                        step(add)

            def first_tile(q, g, slot, stores, pair=0):
                y_low(q)
                for j in range(TAPS):
                    if TAP_ORDER[j] in POOL_TAPS and stores is not None:
                        dve.wait_ge(pool_sum, (q - 1) * len(POOL_TAPS) + POOL_TAPS.index(TAP_ORDER[j]) + 1)
                    tap(q, j, pair, g, slot, ring[j % 7], stores)

            ring = [zb[0], zb[1], yb[1], mb[0], mb[1], mb[2], mb[3]]

            def split(src, hi, lo, tmp=None):
                step(dve.tensor_copy(hi, src))
                settled()
                step(dve.tensor_tensor(lo, src, hi.bitcast(F32), ALU.subtract))

            flush()
            dve.wait_ge(guards, 7)
            first_tile(0, 0, 0, None)
            dve.wait_ge(pool_sum, len(POOL_TAPS))
            first_tile(1, 1, 1, None)
            dve.wait_ge(pool_sum, 2 * len(POOL_TAPS))
            flush()
            per = 2 * (len(VEC_TAPS) - 2)
            with dve.Fori(1, TURNS // 2) as i:
                made[1] = (i - 1, per)
                first_tile(2 * i, 2 * i, 0, 32 * i)
                first_tile(2 * i + 1, 2 * i + 1, 1, 32 * i)
                assert made[2] == per
            made[1] = None
            made[0], made[2] = made[0] + per * (TURNS // 2 - 1), 0
            first_tile(8, 0, 0, 32 * 4, pair=1)

            dve.wait_ge(ld_att, 48)
            split(qkv_raw[:, :], qkv_hi[:, :], qkv_lo[:, :])
            settled()
            dve.memset(u_cls[:, :], 0.0).then_inc(att_w, 1)
            dve.wait_ge(ld_ffn, 112)
            split(wg_raw[:, :], wg_t[:, 0:E], wg_t[:, E:2 * E])
            step(dve.tensor_copy(w1_hi[:, :], w1_raw[:, :]))
            b2h, b2l = b2_tmp[:, 0:P].bitcast(F32R), b2_tmp[:, P:2 * P]
            step(dve.tensor_copy(b2h, b2_raw[:, :]))
            settled()
            step(dve.tensor_copy(w1_raw[:, :].bitcast(F32R), w1_tmp[:, :]))
            step(dve.tensor_tensor(b2l, b2_raw[:, :], b2h.bitcast(F32), ALU.subtract))
            settled()
            step(dve.tensor_tensor(w1_tmp[:, :], w1_tmp[:, :], w1_raw[:, :], ALU.subtract))
            step(dve.tensor_scalar(b2l, b2l, selt[:, 5:6], None, ALU.mult))
            settled()
            step(dve.tensor_scalar(w1_tmp[:, :], w1_tmp[:, :], selt[:, 3:4], None, ALU.mult))
            settled()
            step(dve.scalar_tensor_tensor(b2_t[:, :], b2h.bitcast(F32), selt[:, 4:5], b2l, ALU.mult, ALU.add))
            step(dve.scalar_tensor_tensor(w1_lo[:, :], w1_raw[:, :], selt[:, 2:3], w1_tmp[:, :],
                                          ALU.mult, ALU.add))
            settled()
            dve.memset(u_in[:, 0, :, :], 0.0).then_inc(ffn_w, 1)

            def bc(stat, width):
                return stat[:, 0:width].unsqueeze(2).broadcast_to([P, width, D])

            def norm_centre(src, width):
                step(dve.tensor_reduce(st[:, 0, 0:width], src, AX.X, ALU.add))
                settled()
                step(dve.tensor_scalar(st[:, 1, 0:width], st[:, 0, 0:width], 1.0 / D, None, ALU.mult))
                settled()
                dve.tensor_tensor(xm[:, 0:width, :], src, bc(st[:, 1, :], width), ALU.subtract)\
                   .then_inc(centred, 1)

            def norm_sum(n, width):
                dve.wait_ge(squared, n + 1)
                step(dve.tensor_reduce(st[:, 2, 0:width], sq[:, 0:width, :], AX.X, ALU.add))
                settled()
                dve.tensor_scalar(st[:, 3, 0:width], st[:, 2, 0:width], 1.0 / D, LN_EPS, ALU.mult, ALU.add)\
                   .then_inc(sumsq, 1)

            def norm_split(n, width, hi, lo):
                dve.wait_ge(rstd, n + 1)
                dve.wait_ge(centred, n + 1)
                step(dve.tensor_tensor(zf[:, 0:width, :], xm[:, 0:width, :], bc(st[:, 4, :], width), ALU.mult))
                settled()
                step(dve.tensor_copy(hi, zf[:, 0:width, :]))
                settled()
                dve.tensor_tensor(lo, zf[:, 0:width, :], hi.bitcast(F32), ALU.subtract).then_inc(normed, 1)

            def norm1(t):
                width = 8 if batches(t) == 2 else 1
                dve.wait_ge(ld_h1, upto(t, 32, 32 if width == 8 else 16, 16))
                norm_centre(h1[:, 0:width, :], width)
                norm_sum(2 * t, width)
                if width == 8:
                    dve.wait_ge(zt_ps, 1 if isinstance(t, int) and t == 1 else upto(t - 1, 2, 2, 1))
                norm_split(2 * t, width, ztok[:, 0:width, 0:64], ztok[:, 0:width, 64:128])

            def q_rot(t, a):
                n = chunks(t) * C
                for b in range(batches(t)):
                    dve.wait_ge(q_ps, upto(t, 2, b + 1, 1))
                    tab = tabc_t[:, 0:C] if batches(t) == 1 else tabq_t[:, bass.ds(a * NT, NT)]
                    dve.tensor_tensor(q_t[:, b * NT:b * NT + n], mb[b][:, 0:n], tab, ALU.mult).then_inc(q_sb, 1)

            def k_rotate(t, a, u):
                n = min(2, chunks(t))
                dve.wait_ge(kv_ps, upto(t, 4, u + 1, 1))
                kv = mb[u % 2][:, 0:n * 192].rearrange("p (c k) -> p c k", k=192)[:, :, 0:128]
                if batches(t) == 1:
                    tab = tabc_t[:, C:2 * C]
                else:
                    tab = tabk_t[:, bass.ds(a * NT + 2 * (u % 2) * C, 2 * C)]
                dve.tensor_tensor(km[:, 2 * u:2 * u + n, :], kv, tab.rearrange("p (c k) -> p c k", k=C),
                                  ALU.mult).then_inc(k_mul, 1)

            def k_double(t, b):
                n = chunks(t)
                dve.wait_ge(k_mul, upto(t, 4, 2 * b + 2, 1) if n == CPT else 1)
                src = km[:, CPT * b:CPT * b + n, :]
                dst = kd[:, CPT * b:CPT * b + n, :].rearrange("p c (r d) -> p c r d", r=2)
                one = src[:, :, 0:D].unsqueeze(2).broadcast_to([P, n, 2, D])
                two = src[:, :, D:2 * D].unsqueeze(2).broadcast_to([P, n, 2, D])
                dve.tensor_tensor(dst, one, two, ALU.add).then_inc(k_rot, 1)

            def probs(t, b):
                n = chunks(t)
                dve.wait_ge(sc_ps, upto(t, 2, b + 1, 1))
                mask = causal_t if batches(t) == 2 else ident
                dve.tensor_tensor(prob[:, b * NT:b * NT + n * C].rearrange("p (c k) -> p c k", k=C),
                                  mb[b][:, 0:n * C].rearrange("p (c k) -> p c k", k=C),
                                  mask[:, :].unsqueeze(1).broadcast_to([P, n, C]), ALU.mult).then_inc(prob_sb, 1)

            DECAY = GAMMA ** C
            du = mb[0][:, :].rearrange("p (b c d) -> p c b d", b=2, c=CPT)

            def states(t, first):
                if first:
                    for b in range(2):
                        step(dve.tensor_copy(u_car[:, b, :], u_cls[:, :]))
                    settled()
                dve.wait_ge(du_ps, t + 1)
                for c in range(CPT - 1):
                    prev = u_car[:, :, :] if c == 0 else u_in[:, c, :, :]
                    ins = dve.scalar_tensor_tensor(u_in[:, c + 1, :, :], prev, DECAY, du[:, c], ALU.mult, ALU.add)
                    if c == CPT - 2:
                        ins.then_inc(u_done, 1)
                    else:
                        step(ins)
                        settled()

            def attended(t):
                dve.wait_ge(at_ps, t + 1)
                width = 8 if batches(t) == 2 else 1
                if not (isinstance(t, int) and t == 0):
                    dve.wait_ge(h2_kept, t)
                dve.tensor_tensor(h2n[:, 0:width, :], h1[:, 0:width, :],
                                  mb[1][:, 0:width * D].rearrange("p (c d) -> p c d", d=D), ALU.add)\
                   .then_inc(h2_done, 1)
                if width == 8:
                    dve.wait_ge(u_done, t + 1)
                    step(dve.scalar_tensor_tensor(u_car[:, :, :], u_in[:, CPT - 1, :, :], DECAY, du[:, CPT - 1],
                                                  ALU.mult, ALU.add))

            def norm2_a(t):
                width = 8 if batches(t) == 2 else 1
                dve.wait_ge(h2_done, t + 1)
                norm_centre(h2n[:, 0:width, :], width)

            def norm2_b(t):
                norm_sum(2 * t + 1, 8 if batches(t) == 2 else 1)

            def norm2_c(t):
                width = 8 if batches(t) == 2 else 1
                norm_split(2 * t + 1, width, ftok[:, 0:width, 64:128], ftok[:, 0:width, 0:64])

            def gates(t):
                n = 8 if batches(t) == 2 else 1
                dve.wait_ge(gate_ps, t + 1)
                ps = mb[0][:, 0:n * 16].rearrange("p (c e) -> p c e", e=16)
                g, ge, left, one1, one2 = (gs[:, i, 0:n, :] for i in range(5))
                best, pick = gm[:, 0, 0:n], gm[:, 1, 0:n]

                def wide(x):
                    return x.unsqueeze(2).broadcast_to([P, n, E])

                step(dve.tensor_tensor(g, ps[:, :, 0:E], bg_t[:, :].unsqueeze(1).broadcast_to([P, n, E]), ALU.add))
                settled()
                step(dve.tensor_tensor(g, g, ps[:, :, E:2 * E], ALU.add))
                settled()
                for one in (one1, one2):
                    step(dve.tensor_reduce(best, g, AX.X, ALU.max))
                    settled()
                    step(dve.tensor_tensor(ge, g, wide(best), ALU.is_ge))
                    settled()
                    step(dve.tensor_tensor(ge, ge, order_t[:, :].unsqueeze(1).broadcast_to([P, n, E]), ALU.mult))
                    settled()
                    step(dve.tensor_reduce(pick, ge, AX.X, ALU.max))
                    settled()
                    step(dve.tensor_tensor(one, ge, wide(pick), ALU.is_equal))
                    settled()
                    if one is one1:
                        step(dve.scalar_tensor_tensor(g, one, -3.0e38, g, ALU.mult, ALU.add))
                        settled()
                aux = ftok[:, 0:n, 128:192]
                step(dve.tensor_tensor(left, one1, one2, ALU.add))
                settled()
                step(dve.tensor_scalar(aux[:, :, 0:E], left, -1.0, 1.0, ALU.mult, ALU.add))
                step(dve.tensor_copy(aux[:, :, 10:18], left))
                dve.tensor_copy(aux[:, :, 18:26], left).then_inc(gated, 1)

            def f1_copy(t):
                n = 2 * NT if batches(t) == 2 else C
                if not (isinstance(t, int) and t == 0):
                    dve.wait_ge(hid_ps, upto(t - 1, 16, 16, 8) if not (isinstance(t, int) and t == 1) else 8)
                dve.wait_ge(gt_sb, upto(t, 2, batches(t), 1))
                dve.tensor_copy(f1_t[:, 0:n], g_t[:, 0:n].bitcast(F32)).then_inc(f1_sb, 1)

            def finish(f, b, pair1):
                n = chunks(f)
                if b == 0 and not (isinstance(f, int) and f == 0):
                    dve.wait_ge(stored_out, 32 * f - 16)
                dve.wait_ge(h2_kept, f + 1)
                dve.wait_ge(yt_ps, upto(f, 2, b + 1, 1))
                y = mb[2 + b][:, 0:n * C].rearrange("p (c k) -> p c k", k=C)
                o = o_t[:, CPT * b:CPT * b + n, :]
                step(dve.tensor_tensor(o, h2_of(f, pair1)[:, :, CPT * b:CPT * b + n, :].rearrange("p a c d -> p (a c) d"),
                                       y[:, :, 0:D], ALU.add))
                settled()
                dve.tensor_tensor(o, o, y[:, :, D:2 * D], ALU.add).then_inc(o_done, 1)

            norm1(0)
            q_rot(0, 0)
            k_rotate(0, 0, 0)
            k_double(0, 0)
            probs(0, 0)
            dve.wait_ge(du_ps, 1)
            dve.tensor_scalar(u_cls[:, :], mb[0][:, 0:D], GAMMA, None, ALU.mult).then_inc(u_done, 1)
            attended(0)
            norm2_a(0)
            norm2_b(0)
            norm2_c(0)
            gates(0)
            f1_copy(0)
            dve.wait_ge(ld_tabs, 32)
            norm1(1)
            flush()

            def body(f, a, q):
                t = f + 1
                pair1 = q is None

                def mul(j):
                    if q is not None:
                        if j == 0:
                            dve.wait_ge(pool_sum, q * len(POOL_TAPS))
                        tap(q, j, 1, q - 8, 0, mb[3 - j % 2], 32 * q - 32 * 4)

                if q is not None:
                    y_low(q)
                if a is not None:
                    q_rot(t, a)
                    k_rotate(t, a, 0)
                    k_rotate(t, a, 1)
                    k_double(t, 0)
                mul(0)
                mul(1)
                if a is not None:
                    k_rotate(t, a, 2)
                    k_rotate(t, a, 3)
                    k_double(t, 1)
                mul(2)
                if a is not None:
                    probs(t, 0)
                    probs(t, 1)
                mul(3)
                if a is not None:
                    states(t, isinstance(f, int) and f in (0, 8))
                    attended(t)
                    norm2_a(t)
                mul(4)
                if a is not None:
                    norm2_b(t)
                mul(5)
                if a is not None:
                    norm2_c(t)
                mul(6)
                mul(7)
                if a is not None:
                    gates(t)
                mul(8)
                if a is not None:
                    f1_copy(t)
                for b in range(batches(f)):
                    finish(f, b, pair1)
                if a is not None and not (isinstance(f, int) and f == 15):
                    norm1(t + 1)

            body(0, 0, 9)
            flush()
            for lo_f, hi_f, shift, tiles, per in ((1, 7, 0, True, STEPS_A), (9, 15, 8, False, STEPS_B)):
                with dve.Fori(lo_f, hi_f) as f:
                    made[1] = (f - lo_f, per)
                    body(f, f - shift, f + 9 if tiles else None)
                    assert made[2] == per, made[2]
                made[1] = None
                made[0], made[2] = made[0] + per * (hi_f - lo_f), 0
                if tiles:
                    body(7, 7, None)
                    body(8, 0, None)
                    flush()
            body(15, 7, None)
            body(16, None, None)


STEPS_A = 33
STEPS_B = 31


def kernel(x, cls_tok, L0_tok_conv1_w, L0_tok_conv1_b, L0_tok_bn_gamma, L0_tok_bn_beta, L0_tok_bn_mean,
           L0_tok_bn_var, L0_tok_conv2_w, L0_tok_conv2_b, L0_attn_W_Q, L0_attn_W_K, L0_attn_W_V, L0_ffn_Wg,
           L0_ffn_bg, L0_ffn_W1, L0_ffn_b1, L0_ffn_W2, L0_ffn_b2):
    import numpy as np
    import concourse.bacc as bacc
    from concourse.bass_utils import run_bass_kernel_spmd

    f = np.float32

    def arr(a):
        return np.ascontiguousarray(a)

    w1c, w2c = arr(L0_tok_conv1_w), arr(L0_tok_conv2_w)
    conv1 = np.zeros((P, 3, 2, CR), f)
    for b in range(2):
        conv1[64 * b:64 * b + 64, :, b, :] = w1c.T[:, None, :]
    bnp = np.stack([np.tile(arr(v), 6) for v in (L0_tok_conv1_b, L0_tok_bn_gamma, L0_tok_bn_beta,
                                                 L0_tok_bn_mean, L0_tok_bn_var)], axis=1)
    conv2 = np.zeros((P, TAPS), f)
    conv2[0:96] = np.tile(w2c.T, (6, 1))
    conv2[96:98] = arr(L0_tok_conv2_b)[None]
    colmask = np.zeros((P, P), f)
    for r in range(3):
        for b in range(2):
            colmask[32 * r + 16 * b:32 * r + 16 * b + 16, 64 * b:64 * b + 64] = 1
    colmask[96:98] = 1
    sel = np.zeros((P, 8), f)
    sel[0:64, 0] = 1
    sel[64:96, 1] = 1
    sel[96, 0] = 1
    sel[97, 1] = 1
    sel[64:73, 2] = 1
    sel[0:64, 3] = 1
    sel[73, 3] = 1
    sel[74:82, 4] = 1
    sel[82:90, 5] = 1

    swap = np.arange(D) ^ 1
    wq, wk, wv = arr(L0_attn_W_Q), arr(L0_attn_W_K), arr(L0_attn_W_V)
    one = np.concatenate([wq, wq[:, swap], wk, wk[:, swap], wv], axis=1)
    wqkv = np.concatenate([one, one], axis=0)

    w1 = arr(L0_ffn_W1).transpose(1, 0, 2).reshape(D, E * HID)
    w1hi = np.concatenate([w1, w1], axis=0)
    w1lo = np.zeros((P, E, HID), f)
    w1lo[0:64] = w1.reshape(D, E, HID)
    for e in range(E):
        w1lo[64 + e, e] = OFF
    w1lo[72:74] = arr(L0_ffn_b1)[None]
    w1lo = w1lo.reshape(P, E * HID)
    w2 = arr(arr(L0_ffn_W2).transpose(1, 0, 2).reshape(HID, E * D))
    b2 = np.zeros((P, P), f)
    b2[74:82, 0:D] = arr(L0_ffn_b2)
    b2[82:90, 0:D] = arr(L0_ffn_b2)
    wg = np.concatenate([arr(L0_ffn_Wg)] * 2, axis=0)
    bg = np.tile(arr(L0_ffn_bg)[None], (P, 1))
    order = np.tile(np.arange(E, 0, -1, dtype=f)[None], (P, 1))

    half = np.arange(0, D, 2, dtype=f)
    inv = (f(1.0) / np.power(f(10000.0), half / f(D))).astype(f)
    pos = np.arange(1, SEQ, dtype=f)
    ang = (pos[:, None] * inv[None, :]).astype(f).astype(np.float64)
    base = ((half + f(0.4 * D)) / f(1.4 * D)).astype(np.float64)
    scale = base[None, :] ** (pos[:, None].astype(np.float64) / 512.0)
    local = (np.arange(HW) % C).astype(np.float64)
    sign = np.where(np.arange(D) % 2 == 0, -1.0, 1.0)
    cos = np.repeat(np.cos(ang), 2, axis=1)
    sin = np.repeat(np.sin(ang), 2, axis=1) * sign
    scale = np.repeat(scale, 2, axis=1)
    q_dec = (GAMMA ** local)[:, None]
    k_dec = (GAMMA ** (C - local))[:, None]
    tabq = arr(np.concatenate([cos * scale * q_dec, sin * scale * q_dec], axis=1).T.astype(f))
    tk = np.concatenate([cos / scale * k_dec, sin / scale * k_dec], axis=1).astype(f)
    tabk = arr(tk.reshape(HW // C, C, 2 * D).transpose(1, 0, 2).reshape(P, HW))
    tabc = np.zeros((P, 2 * C), f)
    tabc[0:64, 0:C] = 1
    tabc[:, C:C + D] = 1
    m = np.arange(C)
    causal = np.where(m[:, None] <= m[None, :], GAMMA ** float(-C), 0.0).astype(f)

    arrays = {
        "x": arr(x).reshape(2, P, HW), "cls": arr(cls_tok).reshape(1, D), "conv1": conv1.reshape(P, 96),
        "bnp": arr(bnp), "conv2": conv2, "colmask": colmask, "sel": sel, "wqkv": arr(wqkv), "w1hi": arr(w1hi),
        "w1lo": w1lo, "w2": w2, "b2": b2, "wg": arr(wg), "bg": arr(bg), "tabq": tabq, "tabk": tabk,
        "tabc": tabc, "causal": causal, "order": arr(order),
    }
    nc = bacc.Bacc("TRN2", target_bir_lowering=False, num_devices=1)
    aps = {n: nc.dram_tensor(n, a.shape, F32, kind="ExternalInput").ap() for n, a in arrays.items()}
    out = nc.dram_tensor("out", (NB, SEQ, D), F32, kind="ExternalOutput").ap()
    build(nc, out=out, **aps)
    r = run_bass_kernel_spmd(nc, [arrays], core_ids=[0])
    return r.results[0]["out"]
```

```python
import concourse.bass as bass
from concourse import mybir
from contextlib import ExitStack

F32 = mybir.dt.float32
F32R = mybir.dt.float32r
ACT = mybir.ActivationFunctionType
ALU = mybir.AluOpType
AX = mybir.AxisListType

P = 128
D = 64
NB = 4
IMG = 64
HW = IMG * IMG
SEQ = HW + 1
C = 128
CPT = 4
NT = CPT * C
TURNS = HW // NT
ROWS = NT // IMG
E = 8
HID = 128
TAPS = 9
CR = 16
GAMMA = 0.96875
LN_EPS = 1e-5
BN_EPS = 1e-5
OFF = -(2.0 ** 100)
VEC_TAPS = (4, 0, 1, 2)
POOL_TAPS = (3, 5, 6, 7, 8)
TAP_ORDER = VEC_TAPS + POOL_TAPS


def build(nc, x, cls, conv1, bnp, conv2, colmask, sel, wqkv, w1hi, w1lo, w2, b2, wg, bg,
          tabq, tabk, tabc, causal, order, out):
    ctx = ExitStack()
    with ctx:
        def sb(name, shape, dt=F32):
            return ctx.enter_context(nc.sbuf_tensor(name, shape, dt))

        def sem(name):
            return ctx.enter_context(nc.semaphore(name))

        mixed = nc.dram_tensor("mixed", [2, NB // 2, IMG, IMG, IMG], F32, kind="Internal").ap()

        ident = sb("ident", [P, P])
        selt = sb("selt", [P, 8])
        conv1_t = sb("conv1_t", [P, 96])
        bn_t = sb("bn_t", [96, 5])
        bn_s = sb("bn_s", [96, 4])
        neghalf = sb("neghalf", [P, 8])
        c2 = sb("c2", [P, 4, TAPS])
        mask_cols = sb("mask_cols", [P, P])
        conv2_t = sb("conv2_t", [P, TAPS, P], F32R)
        qkv_raw = sb("qkv_raw", [P, 320])
        qkv_hi = sb("qkv_hi", [P, 320], F32R)
        qkv_lo = sb("qkv_lo", [P, 320], F32R)
        w1_hi = sb("w1_hi", [P, E * HID], F32R)
        w1_lo = sb("w1_lo", [P, E * HID], F32R)
        w2_t = sb("w2_t", [P, E * D])
        b2_t = sb("b2_t", [P, P], F32R)
        wg_raw = sb("wg_raw", [P, E])
        wg_t = sb("wg_t", [P, 2 * E], F32R)
        bg_t = sb("bg_t", [P, E])
        order_t = sb("order_t", [P, E])
        causal_t = sb("causal_t", [P, C])
        tabc_t = sb("tabc_t", [P, 2 * C])
        tabq_t = sb("tabq_t", [P, HW])
        tabk_t = sb("tabk_t", [P, HW])

        ximg = [sb(f"ximg{p}", [P, (IMG + 2) * IMG]) for p in range(2)]
        y_st = sb("y_st", [P, NT], F32R)
        y_f = sb("y_f", [64, NT])
        prod = sb("prod", [P, len(POOL_TAPS) + 1, NT])
        acc = [sb(f"acc{i}", [P, NT]) for i in range(2)]

        h1 = [sb(f"h1_{i}", [P, 8, D]) for i in range(2)]
        xm = sb("xm", [P, 8, D])
        sq = sb("sq", [P, 8, D])
        zf = sq
        st = sb("st", [P, 6, 8])
        ztok = sb("ztok", [P, 8, 2 * D], F32R)
        z_t = sb("z_t", [P, 2 * NT], F32R)
        q_t = sb("q_t", [P, 2 * NT])
        km = sb("km", [P, 8, 2 * D])
        kd = sb("kd", [P, 8, 2 * D])
        v_tok = sb("v_tok", [P, 8, D])
        k_t = sb("k_t", [P, 2 * NT])
        prob = sb("prob", [P, 2 * NT])
        u_cls = sb("u_cls", [P, D])
        u_car = sb("u_car", [P, 2, D])
        u_in = sb("u_in", [P, CPT, 2, D])
        h2n = sb("h2n", [P, 8, D])
        h2 = [sb(f"h2_{i}", [P, 8, D]) for i in range(2)]

        ftok = sb("ftok", [P, 8, 3 * D], F32R)
        f1_t = [sb(f"f1_t{i}", [P, 2 * NT], F32R) for i in range(2)]
        f2_t = [sb(f"f2_t{i}", [P, 2 * NT], F32R) for i in range(2)]
        gs = sb("gs", [P, 6, 8, E])
        gm = sb("gm", [P, 4, 8])
        hid = sb("hid", [P, 8, NT])
        w1_raw = hid[:, 0:2, :].rearrange("p a b -> p (a b)")
        w1_tmp = hid[:, 2:4, :].rearrange("p a b -> p (a b)")
        b2_raw, b2_tmp = hid[:, 4, 0:P], hid[:, 5, 0:2 * P]
        y_sb = sb("y_sb", [P, 2, NT])
        o_t = sb("o_t", [P, 8, D])

        zb = [ctx.enter_context(nc.psum_tensor(f"zb{i}", [P, NT], F32)) for i in range(2)]
        yb = [ctx.enter_context(nc.psum_tensor(f"yb{i}", [P, NT], F32)) for i in range(2)]
        mb = [ctx.enter_context(nc.psum_tensor(f"mb{i}", [P, NT], F32)) for i in range(4)]

        ld_band, ld_x = sem("ld_band"), [sem(f"ld_x{p}") for p in range(2)]
        ld_tok, ld_att, ld_ffn, ld_tabs = sem("ld_tok"), sem("ld_att"), sem("ld_ffn"), sem("ld_tabs")
        ld_h1 = sem("ld_h1")
        stored_tok = [sem(f"stored_tok{i}") for i in range(2)]
        stored_out = sem("stored_out")
        id_steps, pool_steps, vec_steps = sem("id_steps"), sem("pool_steps"), sem("vec_steps")
        guards, bn_scale, bn_bias, conv2_ready = sem("guards"), sem("bn_scale"), sem("bn_bias"), sem("conv2_ready")
        att_w, ffn_w = sem("att_w"), sem("ffn_w")
        conv1_done, relu_done, ylo_done = sem("conv1_done"), sem("relu_done"), sem("ylo_done")
        tap_bc, tap_mul, vec_sum, pool_sum = sem("tap_bc"), sem("tap_mul"), sem("vec_sum"), sem("pool_sum")
        centred, squared, sumsq, rstd, normed = sem("centred"), sem("squared"), sem("sumsq"), sem("rstd"), sem("normed")
        zt_ps, zt_sb, q_ps, q_sb, kv_ps = sem("zt_ps"), sem("zt_sb"), sem("q_ps"), sem("q_sb"), sem("kv_ps")
        k_mul, k_rot, v_sb, kt_ps, kt_sb = sem("k_mul"), sem("k_rot"), sem("v_sb"), sem("kt_ps"), sem("kt_sb")
        sc_ps, prob_sb, du_ps, u_done = sem("sc_ps"), sem("prob_sb"), sem("du_ps"), sem("u_done")
        at_ps, h2_done, h2_kept, du_used = sem("at_ps"), sem("h2_done"), sem("h2_kept"), sem("du_used")
        gt_ps, gt_sb, gate_ps, gate_read = sem("gt_ps"), sem("gt_sb"), sem("gate_ps"), sem("gate_read")
        gated, f2_ps, f2_sb = sem("gated"), sem("f2_ps"), sem("f2_sb")
        hid_ps, hid_sb, y_ps, y_ev, yt_ps, o_done = (
            sem("hid_ps"), sem("hid_sb"), sem("y_ps"), sem("y_ev"), sem("yt_ps"), sem("o_done"))

        def upto(t, per, j, first):
            if is_cls(t):
                return j
            return (t - 1) * per + (first + j)

        def whole(t, per, first):
            return t * per + first

        def is_cls(t):
            return isinstance(t, int) and t == 0

        def is_turn(t, first=0):
            return not isinstance(t, int) or first <= t <= 2 * TURNS

        def batches(t):
            return 1 if is_cls(t) else 2

        def chunks(t):
            return 1 if is_cls(t) else CPT

        def place(t):
            return (t - 1) & (TURNS - 1)

        def ln1(t):
            return 0 if is_cls(t) else 2 * t - 1

        def ln2(t):
            return 2 * t + 1 if isinstance(t, int) and t == 2 * TURNS else 2 * t + 2

        def w_range(k):
            dj = k % 3 - 1
            return max(0, -dj), IMG - max(0, dj)

        block = ctx.enter_context(nc.Block())

        TILE_LOOP, LAST_LOOP = (2, 6), (8, 14)

        def all_bodies(eng, body):
            for f in (-2, -1, 0, 1):
                body(f, f % 2, True)
            with eng.Fori(0, (TILE_LOOP[1] - TILE_LOOP[0]) // 2) as i:
                body(2 * i + TILE_LOOP[0], 0, True)
                body(2 * i + (TILE_LOOP[0] + 1), 1, True)
            for f in (6, 7):
                body(f, f % 2, False)
            with eng.Fori(0, (LAST_LOOP[1] - LAST_LOOP[0]) // 2) as i:
                body(2 * i + LAST_LOOP[0], 0, False)
                body(2 * i + (LAST_LOOP[0] + 1), 1, False)
            for f in (14, 15, 16, 17):
                body(f, f % 2, False)

        @block.sync
        def _(sp):
            sp.dma_start(conv1_t[:, :], conv1).then_inc(ld_tok, 16)
            sp.dma_start(bn_t[:, :], bnp).then_inc(ld_tok, 16)
            sp.dma_start(c2[:, 0, :], conv2).then_inc(ld_tok, 16)
            sp.dma_start(mask_cols[:, :], colmask).then_inc(ld_tok, 16)
            sp.dma_start(selt[:, :], sel).then_inc(ld_tok, 16)
            band = (2 * ROWS + 1) * IMG
            sp.dma_start(ximg[0][:, IMG:IMG + band], x[0][:, 0:band]).then_inc(ld_band, 16)
            sp.dma_start(ximg[0][:, IMG + band:IMG + HW], x[0][:, band:HW]).then_inc(ld_x[0], 16)
            for dst, src in ((qkv_raw, wqkv), (causal_t, causal), (tabc_t, tabc)):
                sp.dma_start(dst[:, :], src).then_inc(ld_att, 16)
            sp.dma_start(h1[0][:, 0, :], cls.to_broadcast([P, D])).then_inc(ld_h1, 16)
            for dst, src in ((w1_raw, w1hi), (w1_tmp, w1lo), (w2_t, w2), (b2_raw, b2), (wg_raw, wg),
                             (bg_t, bg), (order_t, order)):
                sp.dma_start(dst[:, :], src).then_inc(ld_ffn, 16)
            sp.dma_start(ximg[1][:, IMG:IMG + HW], x[1]).then_inc(ld_x[1], 16)
            sp.dma_start(tabq_t[:, :], tabq).then_inc(ld_tabs, 16)
            sp.dma_start(tabk_t[:, :], tabk).then_inc(ld_tabs, 16)

            def store_tok(q, slot, pair, g):
                sp.wait_ge(pool_sum, (q + 1) * len(POOL_TAPS))
                for b in range(2):
                    sp.dma_start(mixed[b, pair, :, bass.ds(g * ROWS, ROWS), :],
                                 acc[slot][64 * b:64 * b + 64, :].rearrange("c (r w) -> c r w", w=IMG))\
                      .then_inc(stored_tok[slot], 16)

            def load_h1(m, par):
                if isinstance(m, int) and m % TURNS == 1:
                    sp.wait_ge(ld_h1, 16)
                    for slot in range(2):
                        sp.wait_ge(stored_tok[slot], 32 * (TURNS // 2) * (1 if m == 1 else 2))
                if not (isinstance(m, int) and m == 1):
                    sp.wait_ge(h2_done, m - 1)
                for b in range(2):
                    src = mixed[b].rearrange("s c h w -> (s c h) w")[bass.ds((m - 1) * NT, NT), :]
                    sp.dma_start(h1[par][:, CPT * b:CPT * b + CPT, :], src.rearrange("(c p) w -> p c w", p=C))\
                      .then_inc(ld_h1, 16)

            def store_out(f):
                for b in range(batches(f)):
                    sp.wait_ge(o_done, upto(f, 2, b + 1, 1))
                    if is_cls(f):
                        sp.dma_start(out[:, 0, :], o_t[0:NB, 0, :]).then_inc(stored_out, 16)
                        continue
                    row = (f - 1) * NT + ((f - 1) // TURNS) * (2 * SEQ - HW) + (b * SEQ + 1)
                    dst = out.rearrange("b s d -> (b s) d")[bass.ds(row, NT), :]
                    sp.dma_start(dst.rearrange("(c p) w -> p c w", p=C), o_t[:, CPT * b:CPT * b + CPT, :])\
                      .then_inc(stored_out, 16)

            with sp.Fori(0, TURNS // 2) as i:
                store_tok(2 * i, 0, 0, 2 * i)
                store_tok(2 * i + 1, 1, 0, 2 * i + 1)

            def body(f, fp, tile):
                if is_turn(f + 3, 1):
                    load_h1(f + 3, 1 - fp)
                if is_turn(f - 1):
                    store_out(f - 1)
                if tile:
                    store_tok(f + 10, fp, 1, f + 2)

            all_bodies(sp, body)
            sp.wait_ge(stored_out, 16 + 32 * 2 * TURNS)

        @block.gpsimd
        def _(pool):
            for p in range(2):
                pool.memset(ximg[p][:, 0:IMG], 0.0).then_inc(guards, 1)
                pool.memset(ximg[p][:, IMG + HW:], 0.0).then_inc(guards, 1)
            pool.memset(ident[:, :], 0.0).then_inc(id_steps, 1)
            pool.memset(ftok[:, :, 128:192].bitcast(F32), 0.0).then_inc(id_steps, 1)
            pool.memset(neghalf[:, :], -0.5).then_inc(id_steps, 1)
            pool.wait_ge(id_steps, 3)
            pool.memset(ftok[:, :, 136:138].bitcast(F32), 1.0).then_inc(guards, 1)
            pool.affine_select(out=ident[:, :], in_=ident[:, :], compare_op=ALU.not_equal, fill=1.0,
                               base=0, pattern=[[-1, P]], channel_multiplier=1).then_inc(guards, 1)
            pool.wait_ge(ld_tok, 80)
            pool.tensor_scalar(bn_s[:, 0:1], bn_t[:, 4:5], 1.0, BN_EPS, ALU.mult, ALU.add).then_inc(pool_steps, 1)
            pool.wait_ge(pool_steps, 1)
            pool.tensor_tensor(bn_s[:, 1:2], bn_s[:, 0:1], neghalf[0:96, 0:1], ALU.pow).then_inc(bn_scale, 1)

            def tile_adds(q, slot):
                for j, k in enumerate(POOL_TAPS):
                    pool.wait_ge(tap_mul, q * TAPS + TAP_ORDER.index(k) + 1)
                    if j == 0:
                        pool.wait_ge(vec_sum, q + 1)
                    else:
                        pool.wait_ge(pool_sum, q * len(POOL_TAPS) + j)
                    lo, hi = w_range(k)
                    a = acc[slot][:, :].rearrange("p (r w) -> p r w", w=IMG)[:, :, lo:hi]
                    pr = prod[:, j, :].rearrange("p (r w) -> p r w", w=IMG)[:, :, lo:hi]
                    pool.tensor_tensor(a, a, pr, ALU.add).then_inc(pool_sum, 1)

            def rsqrt(n, width):
                pool.wait_ge(sumsq, n + 1)
                pool.tensor_tensor(st[:, 4, 0:width], st[:, 3, 0:width], neghalf[:, 0:width], ALU.pow)\
                    .then_inc(rstd, 1)

            with pool.Fori(0, TURNS // 2) as i:
                tile_adds(2 * i, 0)
                tile_adds(2 * i + 1, 1)
            rsqrt(ln1(0), 1)

            def body(f, fp, tile):
                q = f + 10
                if is_turn(f + 1):
                    rsqrt(ln2(f + 1), 1 if is_cls(f + 1) else 8)
                if is_turn(f + 3, 1):
                    rsqrt(ln1(f + 3), 8)
                if tile:
                    tile_adds(q, fp)

            all_bodies(pool, body)

        @block.scalar
        def _(act):
            def relu(q, bank):
                act.wait_ge(conv1_done, q + 1)
                act.activation(y_st[0:96, :], bank[0:96, :], ACT.Relu, bias=bn_s[:, 2:3], scale=bn_s[:, 1:2])\
                   .then_inc(relu_done, 1)
                act.activation(y_f[32:64, :], bank[32:64, :], ACT.Relu, bias=bn_s[32:64, 2:3],
                               scale=bn_s[32:64, 1:2]).then_inc(relu_done, 1)

            def square(n, width):
                act.wait_ge(centred, n + 1)
                act.activation(sq[:, 0:width, :], xm[:, 0:width, :], ACT.Square).then_inc(squared, 1)

            def keep_h2(n, par):
                width = 1 if is_cls(n) else 8
                act.wait_ge(h2_done, n + 1)
                if is_turn(n - 2):
                    act.wait_ge(o_done, whole(n - 2, 2, 1))
                act.activation(h2[par][:, 0:width, :], h2n[:, 0:width, :], ACT.Copy).then_inc(h2_kept, 1)

            def z_out(t):
                for b in range(batches(t)):
                    n = chunks(t) * C
                    act.wait_ge(zt_ps, upto(t, 2, b + 1, 1))
                    act.activation(z_t[:, b * NT:b * NT + n], mb[b][:, 0:n], ACT.Copy).then_inc(zt_sb, 1)

            def v_out(t, u):
                n = min(2, chunks(t))
                act.wait_ge(k_mul, upto(t, 4, u + 1, 1))
                kv = mb[u % 2][:, 0:n * 192].rearrange("p (c k) -> p c k", k=192)
                act.activation(v_tok[:, 2 * u:2 * u + n, :], kv[:, :, 128:192], ACT.Copy).then_inc(v_sb, 1)

            def kt_out(t, b):
                n = chunks(t) * C
                act.wait_ge(kt_ps, upto(t, 2, b + 1, 1))
                act.activation(k_t[:, b * NT:b * NT + n], mb[1 - b][:, 0:n], ACT.Copy).then_inc(kt_sb, 1)

            def gt_out(n, par):
                for b in range(batches(n)):
                    w = chunks(n) * C
                    act.wait_ge(gt_ps, upto(n, 2, b + 1, 1))
                    act.activation(f1_t[par][:, b * NT:b * NT + w], mb[b][:, 0:w], ACT.Copy).then_inc(gt_sb, 1)

            def f2_out(n, par):
                for b in range(batches(n)):
                    w = chunks(n) * C
                    act.wait_ge(f2_ps, upto(n, 2, b + 1, 1))
                    act.activation(f2_t[par][:, b * NT:b * NT + w], mb[1 - b][:, 0:w], ACT.Copy).then_inc(f2_sb, 1)

            def gelu(f, s):
                n = chunks(f) * C
                act.wait_ge(hid_ps, upto(f, 16, s + 1, 8))
                act.activation(hid[:, s % 8, 0:n], zb[s % 2][:, 0:n], ACT.Gelu).then_inc(hid_sb, 1)

            def y_out(f, b):
                n = chunks(f) * C
                act.wait_ge(y_ps, upto(f, 2, b + 1, 1))
                act.activation(y_sb[:, b, 0:n], yb[b][:, 0:n], ACT.Copy).then_inc(y_ev, 1)

            act.wait_ge(bn_bias, 1)
            with act.Fori(0, TURNS // 2) as i:
                relu(2 * i, yb[0])
                relu(2 * i + 1, yb[0])
            square(ln1(0), 1)

            def body(f, fp, tile):
                n, t, m, q = f + 1, f + 2, f + 3, f + 10
                nb = batches(f)

                def gelus(lo, hi):
                    for s in range(lo, hi):
                        if is_turn(f) and s % 2 < nb:
                            gelu(f, s if nb == 2 else s // 2)

                if is_turn(n):
                    square(ln2(n), 1 if is_cls(n) else 8)
                gelus(0, 2)
                if is_turn(t):
                    z_out(t)
                gelus(2, 4)
                if tile:
                    relu(q, mb[2])
                if is_turn(n):
                    keep_h2(n, 1 - fp)
                gelus(4, 5)
                if is_turn(t):
                    v_out(t, 0)
                    if not is_cls(t):
                        v_out(t, 1)
                gelus(5, 6)
                if is_turn(n):
                    gt_out(n, 1 - fp)
                gelus(6, 7)
                if is_turn(t) and not is_cls(t):
                    v_out(t, 2)
                    v_out(t, 3)
                gelus(7, 9)
                if is_turn(t):
                    kt_out(t, 0)
                gelus(9, 10)
                if is_turn(t) and not is_cls(t):
                    kt_out(t, 1)
                gelus(10, 11)
                if is_turn(m, 1):
                    square(ln1(m), 8)
                gelus(11, 12)
                if is_turn(n):
                    f2_out(n, 1 - fp)
                gelus(12, 16)
                if is_turn(f):
                    for b in range(nb):
                        y_out(f, b)

            all_bodies(act, body)

        @block.tensor
        def _(pe):
            def conv1_mm(q, pair, g, bank):
                pe.matmul(bank[0:96, :], conv1_t[:, :], ximg[pair][:, bass.ds(g * NT + IMG, NT)],
                          start=True, stop=True).then_inc(conv1_done, 1)

            def tap_mm(q, j, bank, before):
                if j == 0:
                    pe.wait_ge(ylo_done, q + 1)
                    pe.wait_ge(relu_done, 2 * q + 2)
                if before is not None:
                    pe.wait_ge(tap_mul, before)
                pe.matmul(bank[:, :], conv2_t[:, TAP_ORDER[j], :], y_st[:, :], start=True, stop=True)\
                  .then_inc(tap_bc, 1)

            def z_mm(t):
                n = chunks(t)
                pe.wait_ge(normed, ln1(t) + 1)
                for b in range(batches(t)):
                    if not is_cls(t):
                        pe.wait_ge(h2_done if b == 0 else du_used, t)
                    for c in range(n):
                        k = CPT * b + c
                        last = pe.transpose(mb[b][:, c * C:c * C + C], ztok[:, k, :].bitcast(F32), ident[:, :])
                    last.then_inc(zt_ps, 1)

            def q_mm(t):
                n = chunks(t) * C
                for b in range(batches(t)):
                    pe.wait_ge(zt_sb, upto(t, 2, b + 1, 1))
                    z = z_t[:, b * NT:b * NT + n]
                    pe.matmul(mb[b][:, 0:n], qkv_hi[:, 0:128], z, start=True, stop=False)
                    pe.matmul(mb[b][:, 0:n], qkv_lo[:, 0:128], z, start=False, stop=True).then_inc(q_ps, 1)

            def kv_mm(t, u):
                if u < 2:
                    pe.wait_ge(q_sb, upto(t, 2, u + 1, 1))
                elif isinstance(t, int) and t == 1:
                    pe.wait_ge(gt_sb, 1)
                    pe.wait_ge(v_sb, upto(t, 4, u - 1, 1))
                else:
                    pe.wait_ge(gt_sb, upto(t - 1, 2, u - 1, 1))
                for c in range(min(2, chunks(t))):
                    k = 2 * u + c
                    z = z_t[:, k * C:k * C + C]
                    o = mb[u % 2][:, c * 192:c * 192 + 192]
                    pe.matmul(o, z, qkv_hi[:, 128:320], start=True, stop=False)
                    last = pe.matmul(o, z, qkv_lo[:, 128:320], start=False, stop=True)
                last.then_inc(kv_ps, 1)

            def gt_mm(n, t):
                pe.wait_ge(normed, ln2(n) + 1)
                for b in range(batches(n)):
                    if is_turn(t):
                        pe.wait_ge(v_sb, upto(t, 4, b + 1, 1))
                    elif b == 1:
                        pe.wait_ge(du_used, n + 1)
                    for c in range(chunks(n)):
                        k = CPT * b + c
                        last = pe.transpose(mb[b][:, c * C:c * C + C], ftok[:, k, 0:128].bitcast(F32), ident[:, :])
                    last.then_inc(gt_ps, 1)

            def gate_mm(n, par, t):
                pe.wait_ge(gt_sb, upto(n, 2, batches(n), 1))
                if is_turn(t):
                    pe.wait_ge(v_sb, upto(t, 4, 3, 1))
                for b in range(batches(n)):
                    for c in range(chunks(n)):
                        k = CPT * b + c
                        last = pe.matmul(mb[0][:, k * 16:k * 16 + 16], f1_t[par][:, k * C:k * C + C], wg_t[:, :],
                                         start=True, stop=True)
                last.then_inc(gate_ps, 1)

            def kt_mm(t, b):
                pe.wait_ge(k_rot, upto(t, 2, b + 1, 1))
                if b == 0:
                    pe.wait_ge(v_sb, whole(t, 4, 1))
                else:
                    pe.wait_ge(gate_read, t)
                for c in range(chunks(t)):
                    k = CPT * b + c
                    last = pe.transpose(mb[1 - b][:, c * C:c * C + C], kd[:, k, :], ident[:, :])
                last.then_inc(kt_ps, 1)

            def score_mm(t, b):
                pe.wait_ge(kt_sb, upto(t, 2, b + 1, 1))
                for c in range(chunks(t)):
                    k = CPT * b + c
                    last = pe.matmul(mb[1 - b][:, c * C:c * C + C], k_t[:, k * C:k * C + C],
                                     q_t[:, k * C:k * C + C], start=True, stop=True)
                last.then_inc(sc_ps, 1)

            def f2_mm(n, t):
                pe.wait_ge(gated, n + 1)
                for b in range(batches(n)):
                    if is_turn(t):
                        pe.wait_ge(prob_sb, upto(t, 2, b + 1, 1))
                    for c in range(chunks(n)):
                        k = CPT * b + c
                        last = pe.transpose(mb[1 - b][:, c * C:c * C + C], ftok[:, k, 64:192].bitcast(F32),
                                            ident[:, :])
                    last.then_inc(f2_ps, 1)

            def du_mm(t, n):
                if is_cls(t):
                    pe.wait_ge(prob_sb, 1)
                    pe.matmul(mb[1][:, 0:D], kd[0:1, 0, :], v_tok[0:1, 0, :], start=True, stop=True)\
                      .then_inc(du_ps, 1)
                    return
                pe.wait_ge(f2_sb, upto(n, 2, 1, 1))
                for k in range(8):
                    last = pe.matmul(mb[1][:, k * D:k * D + D], kd[:, k, :], v_tok[:, k, :], start=True, stop=True)
                last.then_inc(du_ps, 1)

            def at_mm(t, n):
                pe.wait_ge(prob_sb, upto(t, 2, batches(t), 1))
                if not is_cls(t):
                    pe.wait_ge(f2_sb, upto(n, 2, batches(n), 1))
                    pe.wait_ge(u_done, t)
                for b in range(batches(t)):
                    for c in range(chunks(t)):
                        k = CPT * b + c
                        o = mb[0][:, k * D:k * D + D]
                        last = pe.matmul(o, prob[:, k * C:k * C + C], v_tok[:, k, :], start=True, stop=is_cls(t))
                        if not is_cls(t):
                            u = u_car[:, b, :] if c == 0 else u_in[:, c, b, :]
                            last = pe.matmul(o, q_t[:, k * C:k * C + C], u, start=False, stop=True)
                last.then_inc(at_ps, 1)

            def w1_mm(f, par, s):
                nb, n = batches(f), chunks(f) * C
                e, b = s // nb, s % nb
                if e == 0:
                    pe.wait_ge(f2_sb, upto(f, 2, b + 1, 1))
                    pe.wait_ge(gt_sb, upto(f, 2, b + 1, 1))
                if is_cls(f):
                    if s >= 2:
                        pe.wait_ge(hid_sb, s - 1)
                else:
                    pe.wait_ge(hid_sb, upto(f, 16, s - 1, 8))
                w = slice(e * HID, e * HID + HID)
                pe.matmul(zb[s % 2][:, 0:n], w1_hi[:, w], f1_t[par][:, b * NT:b * NT + n], start=True, stop=False)
                pe.matmul(zb[s % 2][:, 0:n], w1_lo[:, w], f2_t[par][:, b * NT:b * NT + n], start=False, stop=True)\
                  .then_inc(hid_ps, 1)

            def w2_mm(f, par, j, b):
                nb, n = batches(f), chunks(f) * C
                s0, s1 = 2 * j * nb + b, (2 * j + 1) * nb + b
                if j == 0:
                    if not is_cls(f):
                        pe.wait_ge(y_ev, whole(f - 1, 2, 1))
                    pe.matmul(yb[b][:, 0:n], b2_t[:, :], f2_t[par][:, b * NT:b * NT + n], start=True, stop=False)
                pe.wait_ge(hid_sb, upto(f, 16, s1 + 1, 8))
                pe.matmul(yb[b][0:64, 0:n], w2_t[:, 2 * j * D:2 * j * D + D], hid[:, s0 % 8, 0:n],
                          start=False, stop=j == 3)
                last = pe.matmul(yb[b][64:128, 0:n], w2_t[:, (2 * j + 1) * D:(2 * j + 2) * D],
                                 hid[:, s1 % 8, 0:n], start=False, stop=j == 3)
                if j == 3:
                    last.then_inc(y_ps, 1)

            def yt_mm(f, tiles):
                if not is_cls(f):
                    pe.wait_ge(o_done, whole(f - 1, 2, 1))
                if tiles is not None:
                    pe.wait_ge(tap_mul, TAPS * tiles)
                for b in range(batches(f)):
                    pe.wait_ge(y_ev, upto(f, 2, b + 1, 1))
                    for c in range(chunks(f)):
                        last = pe.transpose(mb[2 + b][:, c * C:c * C + C], y_sb[:, b, c * C:c * C + C], ident[:, :])
                    last.then_inc(yt_ps, 1)

            pe.wait_ge(ld_tok, 80)
            pe.wait_ge(ld_band, 16)
            pe.wait_ge(guards, 7)
            pe.wait_ge(conv2_ready, 1)
            ring = [zb[0], zb[1], yb[1], mb[0], mb[1], mb[2], mb[3]]

            def first_tile(q, checked):
                conv1_mm(q, 0, q, yb[0])
                for j in range(TAPS):
                    if j >= 7:
                        before = q * TAPS + j - 6
                    elif checked:
                        before = (q - 1) * TAPS + (j + 8 if j < 2 else j + 1)
                    else:
                        before = None
                    tap_mm(q, j, ring[j % 7], before)

            first_tile(0, False)
            pe.wait_ge(relu_done, 2)
            first_tile(1, True)
            pe.wait_ge(ld_x[0], 16)
            with pe.Fori(1, TURNS // 2) as i:
                for j in range(2):
                    pe.wait_ge(relu_done, 4 * i + 2 * j)
                    first_tile(2 * i + j, True)
            pe.wait_ge(ld_x[1], 16)
            pe.wait_ge(att_w, 1)
            pe.wait_ge(tap_mul, TURNS * TAPS)

            def body(f, fp, tile):
                n, t, q = f + 1, f + 2, f + 10
                nb = batches(f)

                def slot(s):
                    if not is_turn(f):
                        return
                    if s % 2 < nb:
                        w1_mm(f, fp, s if nb == 2 else s // 2)
                    if s >= 4 and s % 4 < nb:
                        w2_mm(f, fp, s // 4 - 1, s % 4)

                def tap(j):
                    if tile:
                        tap_mm(q, j, mb[3 - j % 2], None if j < 2 else q * TAPS + j - 1)

                slot(0)
                slot(1)
                if is_turn(f - 1):
                    yt_mm(f - 1, q if tile or isinstance(f, int) and f == 6 else None)
                if is_turn(t):
                    z_mm(t)
                slot(2)
                if is_turn(t):
                    q_mm(t)
                slot(3)
                if tile:
                    if is_turn(f - 1):
                        pe.wait_ge(o_done, whole(f - 1, 2, 1))
                    else:
                        pe.wait_ge(tap_mul, q * TAPS)
                    conv1_mm(q, 1, f + 2, mb[2])
                slot(4)
                if is_turn(t):
                    kv_mm(t, 0)
                    if not is_cls(t):
                        kv_mm(t, 1)
                slot(5)
                if is_turn(n):
                    gt_mm(n, t)
                tap(0)
                tap(1)
                slot(6)
                if is_turn(t) and not is_cls(t):
                    kv_mm(t, 2)
                    kv_mm(t, 3)
                tap(2)
                slot(7)
                if is_turn(n):
                    if is_cls(n):
                        pe.wait_ge(ffn_w, 1)
                    gate_mm(n, 1 - fp, t)
                slot(8)
                if is_turn(t):
                    kt_mm(t, 0)
                tap(3)
                slot(9)
                if is_turn(t) and not is_cls(t):
                    kt_mm(t, 1)
                slot(10)
                if is_turn(t):
                    for b in range(batches(t)):
                        score_mm(t, b)
                slot(11)
                if is_turn(n):
                    f2_mm(n, t)
                tap(4)
                tap(5)
                slot(12)
                if is_turn(t):
                    du_mm(t, n)
                slot(13)
                tap(6)
                slot(14)
                if is_turn(t):
                    at_mm(t, n)
                tap(7)
                slot(15)
                tap(8)
                if is_turn(f):
                    for b in range(nb):
                        w2_mm(f, fp, 3, b)

            all_bodies(pe, body)

        @block.vector
        def _(dve):
            made = [0, None, 0]

            def step(ins):
                ins.then_inc(vec_steps, 1)
                made[2] += 1

            def settled():
                if made[1] is None:
                    dve.wait_ge(vec_steps, made[0] + made[2])
                else:
                    i, per = made[1]
                    dve.wait_ge(vec_steps, i * per + (made[0] + made[2]))

            def flush():
                made[0] += made[2]
                made[2] = 0

            step(dve.memset(y_st[96:128, :].bitcast(F32), 0.0))
            settled()
            dve.memset(y_st[96:98, :].bitcast(F32), 1.0).then_inc(guards, 1)
            dve.wait_ge(ld_tok, 80)
            w = c2[:, 0, :]
            hi, lo = c2[:, 1, :].bitcast(F32R), c2[:, 2, :]
            step(dve.tensor_copy(hi, w))
            dve.wait_ge(bn_scale, 1)
            step(dve.tensor_tensor(bn_s[:, 1:2], bn_s[:, 1:2], bn_t[:, 1:2], ALU.mult))
            step(dve.tensor_tensor(bn_s[:, 3:4], bn_t[:, 0:1], bn_t[:, 3:4], ALU.subtract))
            settled()
            step(dve.tensor_tensor(lo, w, hi.bitcast(F32), ALU.subtract))
            dve.scalar_tensor_tensor(bn_s[:, 2:3], bn_s[:, 3:4], bn_s[:, 1:2], bn_t[:, 2:3], ALU.mult, ALU.add)\
               .then_inc(bn_bias, 1)
            settled()
            step(dve.tensor_scalar(lo, lo, selt[:, 1:2], None, ALU.mult))
            settled()
            step(dve.scalar_tensor_tensor(c2[:, 3, :], hi.bitcast(F32), selt[:, 0:1], lo, ALU.mult, ALU.add))
            settled()
            dve.tensor_tensor(conv2_t[:, :, :], c2[:, 3, :].unsqueeze(2).broadcast_to([P, TAPS, P]),
                              mask_cols[:, :].unsqueeze(1).broadcast_to([P, TAPS, P]), ALU.mult)\
               .then_inc(conv2_ready, 1)

            def y_low(q):
                dve.wait_ge(relu_done, 2 * q + 2)
                dve.tensor_tensor(y_st[32:64, :], y_f[32:64, :], y_st[32:64, :].bitcast(F32), ALU.subtract)\
                   .then_inc(ylo_done, 1)

            def tap(q, j, pair, g, slot, bank, stores):
                k = TAP_ORDER[j]
                di = k // 3 - 1
                lo_, hi_ = w_range(k)
                dj = k % 3 - 1
                img = ximg[pair][:, bass.ds((g * ROWS + 1 + di) * IMG, ROWS * IMG)]\
                    .rearrange("p (r w) -> p r w", w=IMG)[:, :, lo_ + dj:hi_ + dj]
                wt = bank[:, :].rearrange("p (r w) -> p r w", w=IMG)[:, :, lo_:hi_]
                dst = acc[slot] if j == 0 else prod[:, POOL_TAPS.index(k) if k in POOL_TAPS else len(POOL_TAPS)]
                view = dst[:, :].rearrange("p (r w) -> p r w", w=IMG)[:, :, lo_:hi_]
                if j == 0 and stores is not None:
                    dve.wait_ge(stored_tok[slot], stores)
                if k in VEC_TAPS[2:]:
                    settled()
                dve.wait_ge(tap_bc, q * TAPS + j + 1)
                dve.tensor_tensor(view, wt, img, ALU.mult).then_inc(tap_mul, 1)
                if k in VEC_TAPS[1:]:
                    dve.wait_ge(tap_mul, q * TAPS + j + 1)
                    settled()
                    a = acc[slot][:, :].rearrange("p (r w) -> p r w", w=IMG)[:, :, lo_:hi_]
                    add = dve.tensor_tensor(a, a, view, ALU.add)
                    if k == VEC_TAPS[-1]:
                        add.then_inc(vec_sum, 1)
                    else:
                        step(add)

            def first_tile(q, g, slot, stores):
                y_low(q)
                for j in range(TAPS):
                    if TAP_ORDER[j] in POOL_TAPS and stores is not None:
                        dve.wait_ge(pool_sum, (q - 1) * len(POOL_TAPS) + POOL_TAPS.index(TAP_ORDER[j]) + 1)
                    tap(q, j, 0, g, slot, ring[j % 7], stores)

            ring = [zb[0], zb[1], yb[1], mb[0], mb[1], mb[2], mb[3]]

            def split(src, hi, lo, tmp=None):
                step(dve.tensor_copy(hi, src))
                settled()
                step(dve.tensor_tensor(lo, src, hi.bitcast(F32), ALU.subtract))

            flush()
            dve.wait_ge(guards, 7)
            first_tile(0, 0, 0, None)
            dve.wait_ge(pool_sum, len(POOL_TAPS))
            first_tile(1, 1, 1, None)
            dve.wait_ge(pool_sum, 2 * len(POOL_TAPS))
            flush()
            per = 2 * (len(VEC_TAPS) - 2)
            with dve.Fori(1, TURNS // 2) as i:
                made[1] = (i - 1, per)
                first_tile(2 * i, 2 * i, 0, 32 * i)
                first_tile(2 * i + 1, 2 * i + 1, 1, 32 * i)
                assert made[2] == per
            made[1] = None
            made[0], made[2] = made[0] + per * (TURNS // 2 - 1), 0

            def bc(stat, width):
                return stat[:, 0:width].unsqueeze(2).broadcast_to([P, width, D])

            def norm_centre(src, width):
                step(dve.tensor_reduce(st[:, 0, 0:width], src, AX.X, ALU.add))
                settled()
                step(dve.tensor_scalar(st[:, 1, 0:width], st[:, 0, 0:width], 1.0 / D, None, ALU.mult))
                settled()
                dve.tensor_tensor(xm[:, 0:width, :], src, bc(st[:, 1, :], width), ALU.subtract)\
                   .then_inc(centred, 1)

            def norm_sum(n, width):
                dve.wait_ge(squared, n + 1)
                step(dve.tensor_reduce(st[:, 2, 0:width], sq[:, 0:width, :], AX.X, ALU.add))
                settled()
                dve.tensor_scalar(st[:, 3, 0:width], st[:, 2, 0:width], 1.0 / D, LN_EPS, ALU.mult, ALU.add)\
                   .then_inc(sumsq, 1)

            def norm_split(n, width, hi, lo):
                dve.wait_ge(rstd, n + 1)
                dve.wait_ge(centred, n + 1)
                step(dve.tensor_tensor(zf[:, 0:width, :], xm[:, 0:width, :], bc(st[:, 4, :], width), ALU.mult))
                settled()
                step(dve.tensor_copy(hi, zf[:, 0:width, :]))
                settled()
                dve.tensor_tensor(lo, zf[:, 0:width, :], hi.bitcast(F32), ALU.subtract).then_inc(normed, 1)

            def q_rot(t):
                n = chunks(t) * C
                for b in range(batches(t)):
                    dve.wait_ge(q_ps, upto(t, 2, b + 1, 1))
                    tab = tabc_t[:, 0:C] if is_cls(t) else tabq_t[:, bass.ds(place(t) * NT, NT)]
                    dve.tensor_tensor(q_t[:, b * NT:b * NT + n], mb[b][:, 0:n], tab, ALU.mult).then_inc(q_sb, 1)

            def k_rotate(t, u):
                n = min(2, chunks(t))
                dve.wait_ge(kv_ps, upto(t, 4, u + 1, 1))
                kv = mb[u % 2][:, 0:n * 192].rearrange("p (c k) -> p c k", k=192)[:, :, 0:128]
                if batches(t) == 1:
                    tab = tabc_t[:, C:2 * C]
                else:
                    tab = tabk_t[:, bass.ds(place(t) * NT + 2 * (u % 2) * C, 2 * C)]
                dve.tensor_tensor(km[:, 2 * u:2 * u + n, :], kv, tab.rearrange("p (c k) -> p c k", k=C),
                                  ALU.mult).then_inc(k_mul, 1)

            def k_double(t, b):
                n = chunks(t)
                dve.wait_ge(k_mul, upto(t, 4, 2 * b + 2, 1) if n == CPT else 1)
                src = km[:, CPT * b:CPT * b + n, :]
                dst = kd[:, CPT * b:CPT * b + n, :].rearrange("p c (r d) -> p c r d", r=2)
                one = src[:, :, 0:D].unsqueeze(2).broadcast_to([P, n, 2, D])
                two = src[:, :, D:2 * D].unsqueeze(2).broadcast_to([P, n, 2, D])
                dve.tensor_tensor(dst, one, two, ALU.add).then_inc(k_rot, 1)

            def probs(t, b):
                n = chunks(t)
                dve.wait_ge(sc_ps, upto(t, 2, b + 1, 1))
                mask = causal_t if batches(t) == 2 else ident
                dve.tensor_tensor(prob[:, b * NT:b * NT + n * C].rearrange("p (c k) -> p c k", k=C),
                                  mb[1 - b][:, 0:n * C].rearrange("p (c k) -> p c k", k=C),
                                  mask[:, :].unsqueeze(1).broadcast_to([P, n, C]), ALU.mult).then_inc(prob_sb, 1)

            DECAY = GAMMA ** C
            du = mb[1][:, :].rearrange("p (b c d) -> p c b d", b=2, c=CPT)

            def states(t):
                if isinstance(t, int) and t % TURNS == 1:
                    for b in range(2):
                        step(dve.tensor_copy(u_car[:, b, :], u_cls[:, :]))
                    settled()
                dve.wait_ge(du_ps, t + 1)
                if is_cls(t):
                    dve.tensor_scalar(u_cls[:, :], mb[1][:, 0:D], GAMMA, None, ALU.mult).then_inc(du_used, 1)
                    return
                for c in range(CPT - 1):
                    prev = u_car[:, :, :] if c == 0 else u_in[:, c, :, :]
                    ins = dve.scalar_tensor_tensor(u_in[:, c + 1, :, :], prev, DECAY, du[:, c], ALU.mult, ALU.add)
                    if c == CPT - 2:
                        ins.then_inc(u_done, 1)
                    else:
                        step(ins)
                        settled()

            def attended(t, par):
                dve.wait_ge(at_ps, t + 1)
                width = 1 if is_cls(t) else 8
                if not is_cls(t):
                    dve.wait_ge(h2_kept, t)
                dve.tensor_tensor(h2n[:, 0:width, :], h1[par][:, 0:width, :],
                                  mb[0][:, 0:width * D].rearrange("p (c d) -> p c d", d=D), ALU.add)\
                   .then_inc(h2_done, 1)
                if not is_cls(t):
                    dve.wait_ge(u_done, t)
                    dve.scalar_tensor_tensor(u_car[:, :, :], u_in[:, CPT - 1, :, :], DECAY, du[:, CPT - 1],
                                             ALU.mult, ALU.add).then_inc(du_used, 1)

            def gates(t):
                n = 8 if batches(t) == 2 else 1
                dve.wait_ge(gate_ps, t + 1)
                ps = mb[0][:, 0:n * 16].rearrange("p (c e) -> p c e", e=16)
                g, ge, left, one1, one2 = (gs[:, i, 0:n, :] for i in range(5))
                best, pick = gm[:, 0, 0:n], gm[:, 1, 0:n]

                def wide(x):
                    return x.unsqueeze(2).broadcast_to([P, n, E])

                step(dve.tensor_tensor(g, ps[:, :, 0:E], bg_t[:, :].unsqueeze(1).broadcast_to([P, n, E]), ALU.add))
                settled()
                dve.tensor_tensor(g, g, ps[:, :, E:2 * E], ALU.add).then_inc(gate_read, 1)
                dve.wait_ge(gate_read, t + 1)
                for one in (one1, one2):
                    step(dve.tensor_reduce(best, g, AX.X, ALU.max))
                    settled()
                    step(dve.tensor_tensor(ge, g, wide(best), ALU.is_ge))
                    settled()
                    step(dve.tensor_tensor(ge, ge, order_t[:, :].unsqueeze(1).broadcast_to([P, n, E]), ALU.mult))
                    settled()
                    step(dve.tensor_reduce(pick, ge, AX.X, ALU.max))
                    settled()
                    step(dve.tensor_tensor(one, ge, wide(pick), ALU.is_equal))
                    settled()
                    if one is one1:
                        step(dve.scalar_tensor_tensor(g, one, -3.0e38, g, ALU.mult, ALU.add))
                        settled()
                aux = ftok[:, 0:n, 128:192]
                step(dve.tensor_tensor(left, one1, one2, ALU.add))
                settled()
                step(dve.tensor_scalar(aux[:, :, 0:E], left, -1.0, 1.0, ALU.mult, ALU.add))
                step(dve.tensor_copy(aux[:, :, 10:18], left))
                dve.tensor_copy(aux[:, :, 18:26], left).then_inc(gated, 1)

            def finish(f, par):
                n = chunks(f)
                if not is_cls(f):
                    dve.wait_ge(stored_out, 32 * f - 16)
                dve.wait_ge(h2_kept, f + 1)
                for b in range(batches(f)):
                    dve.wait_ge(yt_ps, upto(f, 2, b + 1, 1))
                    y = mb[2 + b][:, 0:n * C].rearrange("p (c k) -> p c k", k=C)
                    o = o_t[:, CPT * b:CPT * b + n, :]
                    step(dve.tensor_tensor(o, h2[par][:, CPT * b:CPT * b + n, :], y[:, :, 0:D], ALU.add))
                    settled()
                    dve.tensor_tensor(o, o, y[:, :, D:2 * D], ALU.add).then_inc(o_done, 1)

            dve.wait_ge(ld_att, 48)
            split(qkv_raw[:, :], qkv_hi[:, :], qkv_lo[:, :])
            settled()
            dve.memset(u_cls[:, :], 0.0).then_inc(att_w, 1)
            dve.wait_ge(ld_h1, 16)
            norm_centre(h1[0][:, 0:1, :], 1)
            norm_sum(ln1(0), 1)
            norm_split(ln1(0), 1, ztok[:, 0:1, 0:64], ztok[:, 0:1, 64:128])

            def ffn_weights():
                dve.wait_ge(ld_ffn, 112)
                split(wg_raw[:, :], wg_t[:, 0:E], wg_t[:, E:2 * E])
                step(dve.tensor_copy(w1_hi[:, :], w1_raw[:, :]))
                b2h, b2l = b2_tmp[:, 0:P].bitcast(F32R), b2_tmp[:, P:2 * P]
                step(dve.tensor_copy(b2h, b2_raw[:, :]))
                settled()
                step(dve.tensor_copy(w1_raw[:, :].bitcast(F32R), w1_tmp[:, :]))
                step(dve.tensor_tensor(b2l, b2_raw[:, :], b2h.bitcast(F32), ALU.subtract))
                settled()
                step(dve.tensor_tensor(w1_tmp[:, :], w1_tmp[:, :], w1_raw[:, :], ALU.subtract))
                step(dve.tensor_scalar(b2l, b2l, selt[:, 5:6], None, ALU.mult))
                settled()
                step(dve.tensor_scalar(w1_tmp[:, :], w1_tmp[:, :], selt[:, 3:4], None, ALU.mult))
                settled()
                step(dve.scalar_tensor_tensor(b2_t[:, :], b2h.bitcast(F32), selt[:, 4:5], b2l, ALU.mult, ALU.add))
                step(dve.scalar_tensor_tensor(w1_lo[:, :], w1_raw[:, :], selt[:, 2:3], w1_tmp[:, :],
                                              ALU.mult, ALU.add))
                settled()
                dve.memset(u_in[:, 0, :, :], 0.0).then_inc(ffn_w, 1)

            def body(f, fp, tile):
                n, t, m, q = f + 1, f + 2, f + 3, f + 10
                wn = 1 if is_cls(n) else 8

                def tap_mul_add(j):
                    if tile:
                        if j == 0:
                            dve.wait_ge(pool_sum, q * len(POOL_TAPS))
                        tap(q, j, 1, f + 2, fp, mb[3 - j % 2], 16 * (q - fp))

                if is_turn(n):
                    dve.wait_ge(h2_done, n + 1)
                    norm_centre(h2n[:, 0:wn, :], wn)
                    norm_sum(ln2(n), wn)
                if is_turn(f - 1):
                    finish(f - 1, 1 - fp)
                if is_turn(t):
                    if isinstance(t, int) and t == 1:
                        dve.wait_ge(ld_tabs, 32)
                    q_rot(t)
                if is_turn(n):
                    if not is_cls(n):
                        dve.wait_ge(f2_ps, whole(n - 1, 2, 1))
                    norm_split(ln2(n), wn, ftok[:, 0:wn, 64:128], ftok[:, 0:wn, 0:64])
                if tile:
                    y_low(q)
                if is_turn(t):
                    k_rotate(t, 0)
                    if not is_cls(t):
                        k_rotate(t, 1)
                    k_double(t, 0)
                tap_mul_add(0)
                tap_mul_add(1)
                if is_turn(t) and not is_cls(t):
                    k_rotate(t, 2)
                    k_rotate(t, 3)
                    k_double(t, 1)
                tap_mul_add(2)
                if is_turn(n):
                    gates(n)
                if is_turn(m, 1):
                    dve.wait_ge(ld_h1, whole(m, 32, 16))
                    norm_centre(h1[1 - fp][:, :, :], 8)
                tap_mul_add(3)
                if is_turn(t):
                    for b in range(batches(t)):
                        probs(t, b)
                if is_turn(m, 1):
                    norm_sum(ln1(m), 8)
                tap_mul_add(4)
                tap_mul_add(5)
                if is_turn(t):
                    states(t)
                if is_turn(m, 1):
                    dve.wait_ge(zt_ps, whole(m - 1, 2, 1))
                    norm_split(ln1(m), 8, ztok[:, :, 0:64], ztok[:, :, 64:128])
                tap_mul_add(6)
                if is_turn(t):
                    attended(t, fp)
                tap_mul_add(7)
                tap_mul_add(8)
                if isinstance(f, int) and f == -2:
                    ffn_weights()

            def counted_loop(bodies, tile, per):
                flush()
                with dve.Fori(0, (bodies[1] - bodies[0]) // 2) as i:
                    made[1] = (i, per)
                    body(2 * i + bodies[0], 0, tile)
                    body(2 * i + (bodies[0] + 1), 1, tile)
                    assert made[2] == per, made[2]
                made[1] = None
                made[0], made[2] = made[0] + per * ((bodies[1] - bodies[0]) // 2), 0

            for f in (-2, -1, 0, 1):
                body(f, f % 2, True)
            counted_loop(TILE_LOOP, True, STEPS_TILE)
            for f in (6, 7):
                body(f, f % 2, False)
            counted_loop(LAST_LOOP, False, STEPS_LAST)
            for f in (14, 15, 16, 17):
                body(f, f % 2, False)


STEPS_TILE = 62
STEPS_LAST = 58


def kernel(x, cls_tok, L0_tok_conv1_w, L0_tok_conv1_b, L0_tok_bn_gamma, L0_tok_bn_beta, L0_tok_bn_mean,
           L0_tok_bn_var, L0_tok_conv2_w, L0_tok_conv2_b, L0_attn_W_Q, L0_attn_W_K, L0_attn_W_V, L0_ffn_Wg,
           L0_ffn_bg, L0_ffn_W1, L0_ffn_b1, L0_ffn_W2, L0_ffn_b2):
    import numpy as np
    import concourse.bacc as bacc
    from concourse.bass_utils import run_bass_kernel_spmd

    f = np.float32

    def arr(a):
        return np.ascontiguousarray(a)

    w1c, w2c = arr(L0_tok_conv1_w), arr(L0_tok_conv2_w)
    conv1 = np.zeros((P, 3, 2, CR), f)
    for b in range(2):
        conv1[64 * b:64 * b + 64, :, b, :] = w1c.T[:, None, :]
    bnp = np.stack([np.tile(arr(v), 6) for v in (L0_tok_conv1_b, L0_tok_bn_gamma, L0_tok_bn_beta,
                                                 L0_tok_bn_mean, L0_tok_bn_var)], axis=1)
    conv2 = np.zeros((P, TAPS), f)
    conv2[0:96] = np.tile(w2c.T, (6, 1))
    conv2[96:98] = arr(L0_tok_conv2_b)[None]
    colmask = np.zeros((P, P), f)
    for r in range(3):
        for b in range(2):
            colmask[32 * r + 16 * b:32 * r + 16 * b + 16, 64 * b:64 * b + 64] = 1
    colmask[96:98] = 1
    sel = np.zeros((P, 8), f)
    sel[0:64, 0] = 1
    sel[64:96, 1] = 1
    sel[96, 0] = 1
    sel[97, 1] = 1
    sel[64:73, 2] = 1
    sel[0:64, 3] = 1
    sel[73, 3] = 1
    sel[74:82, 4] = 1
    sel[82:90, 5] = 1

    swap = np.arange(D) ^ 1
    wq, wk, wv = arr(L0_attn_W_Q), arr(L0_attn_W_K), arr(L0_attn_W_V)
    one = np.concatenate([wq, wq[:, swap], wk, wk[:, swap], wv], axis=1)
    wqkv = np.concatenate([one, one], axis=0)

    w1 = arr(L0_ffn_W1).transpose(1, 0, 2).reshape(D, E * HID)
    w1hi = np.concatenate([w1, w1], axis=0)
    w1lo = np.zeros((P, E, HID), f)
    w1lo[0:64] = w1.reshape(D, E, HID)
    for e in range(E):
        w1lo[64 + e, e] = OFF
    w1lo[72:74] = arr(L0_ffn_b1)[None]
    w1lo = w1lo.reshape(P, E * HID)
    w2 = arr(arr(L0_ffn_W2).transpose(1, 0, 2).reshape(HID, E * D))
    b2 = np.zeros((P, P), f)
    b2[74:82, 0:D] = arr(L0_ffn_b2)
    b2[82:90, 0:D] = arr(L0_ffn_b2)
    wg = np.concatenate([arr(L0_ffn_Wg)] * 2, axis=0)
    bg = np.tile(arr(L0_ffn_bg)[None], (P, 1))
    order = np.tile(np.arange(E, 0, -1, dtype=f)[None], (P, 1))

    half = np.arange(0, D, 2, dtype=f)
    inv = (f(1.0) / np.power(f(10000.0), half / f(D))).astype(f)
    pos = np.arange(1, SEQ, dtype=f)
    ang = (pos[:, None] * inv[None, :]).astype(f).astype(np.float64)
    base = ((half + f(0.4 * D)) / f(1.4 * D)).astype(np.float64)
    scale = base[None, :] ** (pos[:, None].astype(np.float64) / 512.0)
    local = (np.arange(HW) % C).astype(np.float64)
    sign = np.where(np.arange(D) % 2 == 0, -1.0, 1.0)
    cos = np.repeat(np.cos(ang), 2, axis=1)
    sin = np.repeat(np.sin(ang), 2, axis=1) * sign
    scale = np.repeat(scale, 2, axis=1)
    q_dec = (GAMMA ** local)[:, None]
    k_dec = (GAMMA ** (C - local))[:, None]
    tabq = arr(np.concatenate([cos * scale * q_dec, sin * scale * q_dec], axis=1).T.astype(f))
    tk = np.concatenate([cos / scale * k_dec, sin / scale * k_dec], axis=1).astype(f)
    tabk = arr(tk.reshape(HW // C, C, 2 * D).transpose(1, 0, 2).reshape(P, HW))
    tabc = np.zeros((P, 2 * C), f)
    tabc[0:64, 0:C] = 1
    tabc[:, C:C + D] = 1
    m = np.arange(C)
    causal = np.where(m[:, None] <= m[None, :], GAMMA ** float(-C), 0.0).astype(f)

    arrays = {
        "x": arr(x).reshape(2, P, HW), "cls": arr(cls_tok).reshape(1, D), "conv1": conv1.reshape(P, 96),
        "bnp": arr(bnp), "conv2": conv2, "colmask": colmask, "sel": sel, "wqkv": arr(wqkv), "w1hi": arr(w1hi),
        "w1lo": w1lo, "w2": w2, "b2": b2, "wg": arr(wg), "bg": arr(bg), "tabq": tabq, "tabk": tabk,
        "tabc": tabc, "causal": causal, "order": arr(order),
    }
    nc = bacc.Bacc("TRN2", target_bir_lowering=False, num_devices=1)
    aps = {n: nc.dram_tensor(n, a.shape, F32, kind="ExternalInput").ap() for n, a in arrays.items()}
    out = nc.dram_tensor("out", (NB, SEQ, D), F32, kind="ExternalOutput").ap()
    build(nc, out=out, **aps)
    r = run_bass_kernel_spmd(nc, [arrays], core_ids=[0])
    return r.results[0]["out"]
```

```python
import concourse.bass as bass
from concourse import mybir
from contextlib import ExitStack

F32 = mybir.dt.float32
F32R = mybir.dt.float32r
ACT = mybir.ActivationFunctionType
ALU = mybir.AluOpType
AX = mybir.AxisListType

P = 128
D = 64
NB = 4
IMG = 64
HW = IMG * IMG
SEQ = HW + 1
C = 128
CPT = 4
NT = CPT * C
TURNS = HW // NT
ROWS = NT // IMG
E = 8
HID = 128
TAPS = 9
CR = 16
GAMMA = 0.96875
LN_EPS = 1e-5
BN_EPS = 1e-5
OFF = -(2.0 ** 100)
TAP_ORDER = (4, 0, 1, 2, 3, 5, 6, 7, 8)
PE_ADDS = 4


def build(nc, x, cls, conv1, bnp, conv2, colmask, sel, wqkv, w1hi, w1lo, w2, b2, wg, bg,
          tabq, tabk, tabc, causal, order, out):
    ctx = ExitStack()
    with ctx:
        def sb(name, shape, dt=F32):
            return ctx.enter_context(nc.sbuf_tensor(name, shape, dt))

        def sem(name):
            return ctx.enter_context(nc.semaphore(name))

        mixed = nc.dram_tensor("mixed", [2, NB // 2, IMG, IMG, IMG], F32, kind="Internal").ap()

        ident = sb("ident", [P, P])
        selt = sb("selt", [P, 8])
        conv1_t = sb("conv1_t", [P, 96])
        bn_t = sb("bn_t", [96, 5])
        bn_s = sb("bn_s", [96, 4])
        neghalf = sb("neghalf", [P, 8])
        c2 = sb("c2", [P, 4, TAPS])
        mask_cols = sb("mask_cols", [P, P])
        conv2_t = sb("conv2_t", [P, TAPS, P], F32R)
        qkv_raw = sb("qkv_raw", [P, 320])
        qkv_hi = sb("qkv_hi", [P, 320], F32R)
        qkv_lo = sb("qkv_lo", [P, 320], F32R)
        w1_hi = sb("w1_hi", [P, E * HID], F32R)
        w1_lo = sb("w1_lo", [P, E * HID], F32R)
        w2_t = sb("w2_t", [P, E * D])
        b2_t = sb("b2_t", [P, P], F32R)
        wg_raw = sb("wg_raw", [P, E])
        wg_t = sb("wg_t", [P, 2 * E], F32R)
        bg_t = sb("bg_t", [P, E])
        order_t = sb("order_t", [P, E])
        causal_t = sb("causal_t", [P, C])
        tabc_t = sb("tabc_t", [P, 2 * C])
        tabq_t = sb("tabq_t", [P, HW])
        tabk_t = sb("tabk_t", [P, HW])

        ximg = [sb(f"ximg{p}", [P, (IMG + 2) * IMG]) for p in range(2)]
        y_st = [sb(f"y_st{i}", [P, NT], F32R) for i in range(2)]
        y_f = sb("y_f", [64, NT])
        prod = sb("prod", [P, TAPS, NT])
        acc = [sb(f"acc{i}", [P, NT]) for i in range(2)]

        h1 = [sb(f"h1_{i}", [P, 8, D]) for i in range(2)]
        xm = sb("xm", [P, 8, D])
        sq = sb("sq", [P, 8, D])
        st = sb("st", [P, 6, 8])
        ztok = sb("ztok", [P, 8, D])
        z_t = sb("z_t", [P, 2 * NT], F32R)
        q_t = sb("q_t", [P, 2 * NT])
        km = sb("km", [P, 8, 2 * D])
        kd = sb("kd", [P, 8, 2 * D])
        v_tok = sb("v_tok", [P, 8, D])
        k_t = sb("k_t", [P, 2 * NT])
        prob = sb("prob", [P, 2 * NT])
        u_cls = sb("u_cls", [P, D])
        u_car = sb("u_car", [P, 2, D])
        u_in = sb("u_in", [P, CPT, 2, D])
        h2n = sb("h2n", [P, 8, D])
        h2 = [sb(f"h2_{i}", [P, 8, D]) for i in range(2)]

        z2tok = sb("z2tok", [P, 8, D])
        aux = sb("aux", [P, 8, D])
        f1_t = [sb(f"f1_t{i}", [P, 2 * NT], F32R) for i in range(2)]
        f2_t = [sb(f"f2_t{i}", [P, 2 * NT], F32R) for i in range(2)]
        gs = sb("gs", [P, 6, 8, E])
        gm = sb("gm", [P, 4, 8])
        hid = sb("hid", [P, 8, NT])
        w1_raw = hid[:, 0:2, :].rearrange("p a b -> p (a b)")
        w1_tmp = hid[:, 2:4, :].rearrange("p a b -> p (a b)")
        b2_raw, b2_tmp = hid[:, 4, 0:P], hid[:, 5, 0:2 * P]
        y_sb = sb("y_sb", [P, 2, NT])
        o_t = sb("o_t", [P, 8, D])

        zb = [ctx.enter_context(nc.psum_tensor(f"zb{i}", [P, NT], F32)) for i in range(2)]
        yb = [ctx.enter_context(nc.psum_tensor(f"yb{i}", [P, NT], F32)) for i in range(2)]
        mb = [ctx.enter_context(nc.psum_tensor(f"mb{i}", [P, NT], F32)) for i in range(4)]

        ld_band, ld_x = sem("ld_band"), [sem(f"ld_x{p}") for p in range(2)]
        ld_tok, ld_att, ld_ffn, ld_tabs = sem("ld_tok"), sem("ld_att"), sem("ld_ffn"), sem("ld_tabs")
        ld_h1 = sem("ld_h1")
        stored_tok = [sem(f"stored_tok{i}") for i in range(2)]
        stored_out = sem("stored_out")
        id_steps, pool_steps, vec_steps = sem("id_steps"), sem("pool_steps"), sem("vec_steps")
        guards, bn_scale, bn_bias, conv2_ready = sem("guards"), sem("bn_scale"), sem("bn_bias"), sem("conv2_ready")
        att_w, ffn_w = sem("att_w"), sem("ffn_w")
        conv1_done, relu_done, ylo_done = sem("conv1_done"), sem("relu_done"), sem("ylo_done")
        tap_bc, tap_mul, pe_sum, part_sum = sem("tap_bc"), sem("tap_mul"), sem("pe_sum"), sem("part_sum")
        pool_sum = sem("pool_sum")
        centred, squared, sumsq, rstd, normed = sem("centred"), sem("squared"), sem("sumsq"), sem("rstd"), sem("normed")
        zt_ps, z_hi, z_lo, q_ps, q_sb, kv_ps = (
            sem("zt_ps"), sem("z_hi"), sem("z_lo"), sem("q_ps"), sem("q_sb"), sem("kv_ps"))
        k_mul, k_rot, v_sb, kt_ps, kt_sb = sem("k_mul"), sem("k_rot"), sem("v_sb"), sem("kt_ps"), sem("kt_sb")
        sc_ps, prob_sb, du_ps, u_done = sem("sc_ps"), sem("prob_sb"), sem("du_ps"), sem("u_done")
        at_ps, h2_done, h2_kept, du_used = sem("at_ps"), sem("h2_done"), sem("h2_kept"), sem("du_used")
        gt_ps, f1_hi, f1_lo, gate_ps, gate_read = (
            sem("gt_ps"), sem("f1_hi"), sem("f1_lo"), sem("gate_ps"), sem("gate_read"))
        gated, f2_ps, f2_sb = sem("gated"), sem("f2_ps"), sem("f2_sb")
        hid_ps, hid_sb, y_ps, y_ev, yt_ps, o_done = (
            sem("hid_ps"), sem("hid_sb"), sem("y_ps"), sem("y_ev"), sem("yt_ps"), sem("o_done"))

        def upto(t, per, j, first):
            if is_cls(t):
                return j
            return (t - 1) * per + (first + j)

        def whole(t, per, first):
            return t * per + first

        def is_cls(t):
            return isinstance(t, int) and t == 0

        def pool_adds(q, first):
            if first:
                return (TAPS - PE_ADDS) * q
            return (TAPS - 1) * q - TURNS * (PE_ADDS - 1)

        def is_turn(t, first=0):
            return not isinstance(t, int) or first <= t <= 2 * TURNS

        def batches(t):
            return 1 if is_cls(t) else 2

        def chunks(t):
            return 1 if is_cls(t) else CPT

        def place(t):
            return (t - 1) & (TURNS - 1)

        def of_batch(tile, b, n=CPT):
            return tile[:, :, :].rearrange("p (c b) d -> p b c d", b=2)[:, b, 0:n, :]

        def ln1(t):
            return 0 if is_cls(t) else 2 * t - 1

        def ln2(t):
            return 2 * t + 1 if isinstance(t, int) and t == 2 * TURNS else 2 * t + 2

        def w_range(k):
            dj = k % 3 - 1
            return max(0, -dj), IMG - max(0, dj)

        block = ctx.enter_context(nc.Block())

        TILE_LOOP, LAST_LOOP = (2, 6), (8, 14)

        def all_bodies(eng, body):
            for f in (-2, -1, 0, 1):
                body(f, f % 2, True)
            with eng.Fori(0, (TILE_LOOP[1] - TILE_LOOP[0]) // 2) as i:
                body(2 * i + TILE_LOOP[0], 0, True)
                body(2 * i + (TILE_LOOP[0] + 1), 1, True)
            for f in (6, 7):
                body(f, f % 2, False)
            with eng.Fori(0, (LAST_LOOP[1] - LAST_LOOP[0]) // 2) as i:
                body(2 * i + LAST_LOOP[0], 0, False)
                body(2 * i + (LAST_LOOP[0] + 1), 1, False)
            for f in (14, 15, 16, 17):
                body(f, f % 2, False)

        kv_bank = [mb[1], mb[0], mb[1], mb[0]]
        tap_bank = [zb[0], zb[1], mb[0], mb[1], mb[2]]
        part_bank = [yb[1], mb[3]]

        @block.sync
        def _(sp):
            sp.dma_start(conv1_t[:, :], conv1).then_inc(ld_tok, 16)
            sp.dma_start(bn_t[:, :], bnp).then_inc(ld_tok, 16)
            sp.dma_start(c2[:, 0, :], conv2).then_inc(ld_tok, 16)
            sp.dma_start(mask_cols[:, :], colmask).then_inc(ld_tok, 16)
            sp.dma_start(selt[:, :], sel).then_inc(ld_tok, 16)
            sp.dma_start(h1[0][:, 0, :], cls.to_broadcast([P, D])).then_inc(ld_h1, 16)
            band = (2 * ROWS + 1) * IMG
            sp.dma_start(ximg[0][:, IMG:IMG + band], x[0][:, 0:band]).then_inc(ld_band, 16)
            sp.dma_start(ximg[0][:, IMG + band:IMG + HW], x[0][:, band:HW]).then_inc(ld_x[0], 16)
            for dst, src in ((qkv_raw, wqkv), (causal_t, causal), (tabc_t, tabc)):
                sp.dma_start(dst[:, :], src).then_inc(ld_att, 16)
            for dst, src in ((w1_raw, w1hi), (w1_tmp, w1lo), (w2_t, w2), (b2_raw, b2), (wg_raw, wg),
                             (bg_t, bg), (order_t, order)):
                sp.dma_start(dst[:, :], src).then_inc(ld_ffn, 16)
            sp.dma_start(ximg[1][:, IMG:IMG + HW], x[1]).then_inc(ld_x[1], 16)
            sp.dma_start(tabq_t[:, :], tabq).then_inc(ld_tabs, 16)
            sp.dma_start(tabk_t[:, :], tabk).then_inc(ld_tabs, 16)

            def store_tok(q, slot, pair, g):
                sp.wait_ge(pool_sum, pool_adds(q + 1, pair == 0))
                for b in range(2):
                    sp.dma_start(mixed[b, pair, :, bass.ds(g * ROWS, ROWS), :],
                                 acc[slot][64 * b:64 * b + 64, :].rearrange("c (r w) -> c r w", w=IMG))\
                      .then_inc(stored_tok[slot], 16)

            def load_h1(m, par):
                if isinstance(m, int) and m % TURNS == 1:
                    sp.wait_ge(ld_h1, 16)
                    for slot in range(2):
                        sp.wait_ge(stored_tok[slot], 32 * (TURNS // 2) * (1 if m == 1 else 2))
                if not (isinstance(m, int) and m == 1):
                    sp.wait_ge(h2_done, m - 1)
                for b in range(2):
                    src = mixed[b].rearrange("s c h w -> (s c h) w")[bass.ds((m - 1) * NT, NT), :]
                    sp.dma_start(of_batch(h1[par], b), src.rearrange("(c p) w -> p c w", p=C))\
                      .then_inc(ld_h1, 16)

            def store_out(f):
                for b in range(batches(f)):
                    sp.wait_ge(o_done, upto(f, 2, b + 1, 1))
                    if is_cls(f):
                        sp.dma_start(out[:, 0, :], o_t[0:NB, 0, :]).then_inc(stored_out, 16)
                        continue
                    row = (f - 1) * NT + ((f - 1) // TURNS) * (2 * SEQ - HW) + (b * SEQ + 1)
                    dst = out.rearrange("b s d -> (b s) d")[bass.ds(row, NT), :]
                    sp.dma_start(dst.rearrange("(c p) w -> p c w", p=C), of_batch(o_t, b))\
                      .then_inc(stored_out, 16)

            with sp.Fori(0, TURNS // 2) as i:
                store_tok(2 * i, 0, 0, 2 * i)
                store_tok(2 * i + 1, 1, 0, 2 * i + 1)

            def body(f, fp, tile):
                if is_turn(f + 3, 1):
                    load_h1(f + 3, 1 - fp)
                if is_turn(f - 1):
                    store_out(f - 1)
                if tile:
                    store_tok(f + 10, fp, 1, f + 2)

            all_bodies(sp, body)
            sp.wait_ge(stored_out, 16 + 32 * 2 * TURNS)

        @block.gpsimd
        def _(pool):
            for p in range(2):
                pool.memset(ximg[p][:, 0:IMG], 0.0).then_inc(guards, 1)
                pool.memset(ximg[p][:, IMG + HW:], 0.0).then_inc(guards, 1)
            pool.memset(ident[:, :], 0.0).then_inc(id_steps, 1)
            pool.memset(aux[:, :, :], 0.0).then_inc(id_steps, 1)
            pool.memset(neghalf[:, :], -0.5).then_inc(id_steps, 1)
            pool.wait_ge(id_steps, 3)
            pool.memset(aux[:, :, 8:10], 1.0).then_inc(guards, 1)
            pool.affine_select(out=ident[:, :], in_=ident[:, :], compare_op=ALU.not_equal, fill=1.0,
                               base=0, pattern=[[-1, P]], channel_multiplier=1).then_inc(guards, 1)
            pool.wait_ge(ld_tok, 80)
            pool.tensor_scalar(bn_s[:, 0:1], bn_t[:, 4:5], 1.0, BN_EPS, ALU.mult, ALU.add).then_inc(pool_steps, 1)
            pool.wait_ge(pool_steps, 1)
            pool.tensor_tensor(bn_s[:, 1:2], bn_s[:, 0:1], neghalf[0:96, 0:1], ALU.pow).then_inc(bn_scale, 1)

            def tile_adds(q, slot, lo_j, hi_j, first=False):
                for j in range(lo_j, hi_j):
                    pool.wait_ge(tap_mul, q * TAPS + j + 1)
                    if j > (PE_ADDS if first else 1):
                        pool.wait_ge(pool_sum, pool_adds(q, first) + (j - (PE_ADDS if first else 1)))
                    elif first:
                        pool.wait_ge(part_sum, q + 1)
                    lo, hi = w_range(TAP_ORDER[j])
                    a = acc[slot][:, :].rearrange("p (r w) -> p r w", w=IMG)[:, :, lo:hi]
                    pr = prod[:, j, :].rearrange("p (r w) -> p r w", w=IMG)[:, :, lo:hi]
                    pool.tensor_tensor(a, a, pr, ALU.add).then_inc(pool_sum, 1)

            def rsqrt(n, width):
                pool.wait_ge(sumsq, n + 1)
                pool.tensor_tensor(st[:, 4, 0:width], st[:, 3, 0:width], neghalf[:, 0:width], ALU.pow)\
                    .then_inc(rstd, 1)

            rsqrt(ln1(0), 1)
            with pool.Fori(0, TURNS // 2) as i:
                tile_adds(2 * i, 0, PE_ADDS, TAPS, True)
                tile_adds(2 * i + 1, 1, PE_ADDS, TAPS, True)

            def body(f, fp, tile):
                q = f + 10
                if is_turn(f + 1):
                    rsqrt(ln2(f + 1), 1 if is_cls(f + 1) else 8)
                if tile:
                    tile_adds(q, fp, 1, 4)
                if is_turn(f + 3, 1):
                    rsqrt(ln1(f + 3), 8)
                if tile:
                    tile_adds(q, fp, 4, TAPS)

            all_bodies(pool, body)

        @block.scalar
        def _(act):
            def relu(q, slot, bank):
                act.wait_ge(conv1_done, q + 1)
                act.activation(y_st[slot][0:96, :], bank[0:96, :], ACT.Relu, bias=bn_s[:, 2:3], scale=bn_s[:, 1:2])\
                   .then_inc(relu_done, 1)
                act.activation(y_f[32:64, :], bank[32:64, :], ACT.Relu, bias=bn_s[32:64, 2:3],
                               scale=bn_s[32:64, 1:2]).then_inc(relu_done, 1)

            def square(n, width):
                act.wait_ge(centred, n + 1)
                act.activation(sq[:, 0:width, :], xm[:, 0:width, :], ACT.Square).then_inc(squared, 1)

            def keep_h2(n, par):
                width = 1 if is_cls(n) else 8
                act.wait_ge(h2_done, n + 1)
                if is_turn(n - 2):
                    act.wait_ge(o_done, whole(n - 2, 2, 1))
                act.activation(h2[par][:, 0:width, :], h2n[:, 0:width, :], ACT.Copy).then_inc(h2_kept, 1)

            def z_high(t):
                n = chunks(t) * C
                act.wait_ge(zt_ps, t + 1)
                for b in range(batches(t)):
                    half = slice(D * b, D * b + D)
                    act.activation(z_t[half, b * NT:b * NT + n], mb[0][half, 0:n], ACT.Copy).then_inc(z_hi, 1)

            def v_out(t, u):
                n = min(2, chunks(t))
                act.wait_ge(k_mul, upto(t, 4, u + 1, 1))
                kv = kv_bank[u][:, 0:n * 192].rearrange("p (c k) -> p c k", k=192)
                act.activation(v_tok[:, 2 * u:2 * u + n, :], kv[:, :, 128:192], ACT.Copy).then_inc(v_sb, 1)

            def kt_out(t, b):
                n = chunks(t) * C
                act.wait_ge(kt_ps, upto(t, 2, b + 1, 1))
                act.activation(k_t[:, b * NT:b * NT + n], mb[b][:, 0:n], ACT.Copy).then_inc(kt_sb, 1)

            def f1_high(n, par):
                w = chunks(n) * C
                act.wait_ge(gt_ps, n + 1)
                for b in range(batches(n)):
                    half = slice(D * b, D * b + D)
                    act.activation(f1_t[par][half, b * NT:b * NT + w], mb[1][half, 0:w], ACT.Copy).then_inc(f1_hi, 1)

            def f2_high(n, par):
                w = chunks(n) * C
                act.wait_ge(f1_hi, whole(n, 2, 1))
                for b in range(batches(n)):
                    cols = slice(b * NT, b * NT + w)
                    act.activation(f2_t[par][0:D, cols], f1_t[par][D * b:D * b + D, cols].bitcast(F32), ACT.Copy)\
                       .then_inc(f2_sb, 1)

            def f2_out(n, par):
                w = chunks(n) * C
                act.wait_ge(f2_ps, n + 1)
                for b in range(batches(n)):
                    act.activation(f2_t[par][D:2 * D, b * NT:b * NT + w], mb[0][D * b:D * b + D, 0:w], ACT.Copy)\
                       .then_inc(f2_sb, 1)

            def gelu(f, s):
                n = chunks(f) * C
                act.wait_ge(hid_ps, upto(f, 16, s + 1, 8))
                act.activation(hid[:, s % 8, 0:n], zb[s % 2][:, 0:n], ACT.Gelu).then_inc(hid_sb, 1)

            def y_out(f, b):
                n = chunks(f) * C
                act.wait_ge(y_ps, upto(f, 2, b + 1, 1))
                act.activation(y_sb[:, b, 0:n], yb[b][:, 0:n], ACT.Copy).then_inc(y_ev, 1)

            act.wait_ge(bn_bias, 1)
            square(ln1(0), 1)

            def part_out(q, slot, stores):
                act.wait_ge(pe_sum, (q + 1) * PE_ADDS)
                if stores is not None:
                    act.wait_ge(stored_tok[slot], stores)
                act.activation(acc[slot][:, :], part_bank[slot][:, :], ACT.Copy).then_inc(part_sum, 1)

            def first_tile(q, slot, stores, last=False):
                if not last:
                    relu(q + 1, 1 - slot, yb[0])
                part_out(q, slot, stores)

            relu(0, 0, yb[0])
            first_tile(0, 0, None)
            first_tile(1, 1, None)
            with act.Fori(1, TURNS // 2 - 1) as i:
                first_tile(2 * i, 0, 32 * i)
                first_tile(2 * i + 1, 1, 32 * i)
            first_tile(TURNS - 2, 0, 16 * (TURNS - 2))
            first_tile(TURNS - 1, 1, 16 * (TURNS - 2), last=True)
            z_high(0)

            def body(f, fp, tile):
                n, t, m, q = f + 1, f + 2, f + 3, f + 10
                nb = batches(f)

                def gelus(lo, hi):
                    for s in range(lo, hi):
                        if is_turn(f) and s % 2 < nb:
                            gelu(f, s if nb == 2 else s // 2)

                gelus(0, 2)
                if is_turn(n):
                    square(ln2(n), 1 if is_cls(n) else 8)
                gelus(2, 5)
                if is_turn(t):
                    v_out(t, 0)
                    if not is_cls(t):
                        v_out(t, 1)
                if tile:
                    relu(q, fp, mb[2])
                gelus(5, 6)
                if is_turn(t) and not is_cls(t):
                    v_out(t, 2)
                    v_out(t, 3)
                gelus(6, 7)
                if is_turn(n):
                    f1_high(n, 1 - fp)
                gelus(7, 9)
                if is_turn(n):
                    f2_high(n, 1 - fp)
                gelus(9, 10)
                if is_turn(t):
                    kt_out(t, 0)
                if is_turn(n):
                    keep_h2(n, 1 - fp)
                if is_turn(t) and not is_cls(t):
                    kt_out(t, 1)
                gelus(10, 13)
                if is_turn(n):
                    f2_out(n, 1 - fp)
                if is_turn(m, 1):
                    square(ln1(m), 8)
                gelus(13, 16)
                if is_turn(f):
                    y_out(f, 0)
                if is_turn(m, 1):
                    z_high(m)
                if is_turn(f) and nb == 2:
                    y_out(f, 1)

            all_bodies(act, body)

        @block.tensor
        def _(pe):
            def conv1_mm(q, pair, g, bank):
                pe.matmul(bank[0:96, :], conv1_t[:, :], ximg[pair][:, bass.ds(g * NT + IMG, NT)],
                          start=True, stop=True).then_inc(conv1_done, 1)

            def tap_mm(q, slot, j, bank, before):
                if j == 0:
                    pe.wait_ge(ylo_done, q + 1)
                    pe.wait_ge(relu_done, 2 * q + 2)
                if before is not None:
                    pe.wait_ge(tap_mul, before)
                pe.matmul(bank[:, :], conv2_t[:, TAP_ORDER[j], :], y_st[slot][:, :], start=True, stop=True)\
                  .then_inc(tap_bc, 1)

            def token_t(bank, tok, n):
                if n == 1:
                    return pe.transpose(bank[0:D, 0:C], tok[:, 0, :], ident[:, :])
                for c in range(n):
                    last = pe.transpose(bank[:, c * C:c * C + C], tok[:, 2 * c:2 * c + 2, :].rearrange("p b d -> p (b d)"),
                                        ident[:, :])
                return last

            def z_mm(t):
                pe.wait_ge(normed, ln1(t) + 1)
                if not is_cls(t):
                    pe.wait_ge(h2_done, t)
                token_t(mb[0], ztok, chunks(t)).then_inc(zt_ps, 1)

            def q_mm(t):
                n = chunks(t) * C
                for b in range(batches(t)):
                    if b == 0 and not is_cls(t):
                        pe.wait_ge(du_used, t)
                    pe.wait_ge(z_lo, upto(t, 2, b + 1, 1))
                    z = z_t[:, b * NT:b * NT + n]
                    o = mb[1 - b][:, 0:n]
                    pe.matmul(o, qkv_hi[:, 0:128], z, start=True, stop=False)
                    pe.matmul(o, qkv_lo[:, 0:128], z, start=False, stop=True).then_inc(q_ps, 1)

            def kv_mm(t, u):
                if u < 2:
                    pe.wait_ge(q_sb, upto(t, 2, u + 1, 1))
                else:
                    pe.wait_ge(v_sb, upto(t, 4, u - 1, 1))
                for c in range(min(2, chunks(t))):
                    k = 2 * u + c
                    z = z_t[:, k * C:k * C + C]
                    o = kv_bank[u][:, c * 192:c * 192 + 192]
                    pe.matmul(o, z, qkv_hi[:, 128:320], start=True, stop=False)
                    last = pe.matmul(o, z, qkv_lo[:, 128:320], start=False, stop=True)
                last.then_inc(kv_ps, 1)

            def gt_mm(n, t):
                pe.wait_ge(normed, ln2(n) + 1)
                if is_turn(t):
                    pe.wait_ge(v_sb, upto(t, 4, 3, 1))
                else:
                    pe.wait_ge(du_used, n + 1)
                token_t(mb[1], z2tok, chunks(n)).then_inc(gt_ps, 1)

            def gate_mm(n, par):
                pe.wait_ge(f1_lo, whole(n, 2, 1))
                for b in range(batches(n)):
                    for c in range(chunks(n)):
                        k, m = 2 * c + b, CPT * b + c
                        last = pe.matmul(mb[1][:, k * 16:k * 16 + 16], f1_t[par][:, m * C:m * C + C], wg_t[:, :],
                                         start=True, stop=True)
                last.then_inc(gate_ps, 1)

            def kt_mm(t, b):
                pe.wait_ge(k_rot, upto(t, 2, b + 1, 1))
                if b == 0:
                    pe.wait_ge(v_sb, whole(t, 4, 1))
                else:
                    pe.wait_ge(gate_read, t)
                for c in range(chunks(t)):
                    k = CPT * b + c
                    last = pe.transpose(mb[b][:, c * C:c * C + C], kd[:, k, :], ident[:, :])
                last.then_inc(kt_ps, 1)

            def score_mm(t, b):
                pe.wait_ge(kt_sb, upto(t, 2, b + 1, 1))
                for c in range(chunks(t)):
                    k = CPT * b + c
                    last = pe.matmul(mb[b][:, c * C:c * C + C], k_t[:, k * C:k * C + C],
                                     q_t[:, k * C:k * C + C], start=True, stop=True)
                last.then_inc(sc_ps, 1)

            def f2_mm(n, t):
                pe.wait_ge(gated, n + 1)
                if is_turn(t):
                    pe.wait_ge(prob_sb, upto(t, 2, 1, 1))
                token_t(mb[0], aux, chunks(n)).then_inc(f2_ps, 1)

            def du_mm(t):
                pe.wait_ge(prob_sb, whole(t, 2, 1))
                if is_cls(t):
                    pe.matmul(mb[1][:, 0:D], kd[0:1, 0, :], v_tok[0:1, 0, :], start=True, stop=True)\
                      .then_inc(du_ps, 1)
                    return
                for k in range(8):
                    for half in (0, D):
                        last = pe.matmul(mb[1][half:half + D, k * D:k * D + D], kd[:, k, half:half + D],
                                         v_tok[:, k, :], start=True, stop=True)
                last.then_inc(du_ps, 1)

            def at_mm(t, n):
                pe.wait_ge(prob_sb, upto(t, 2, batches(t), 1))
                if not is_cls(t):
                    pe.wait_ge(f2_sb, whole(n, 4, 2))
                    pe.wait_ge(u_done, t)
                for b in range(batches(t)):
                    for c in range(chunks(t)):
                        k, m = CPT * b + c, 2 * c + b
                        o = mb[0][:, m * D:m * D + D]
                        last = pe.matmul(o, prob[:, k * C:k * C + C], v_tok[:, k, :], start=True, stop=is_cls(t))
                        if not is_cls(t):
                            u = u_car[:, b, :] if c == 0 else u_in[:, c, b, :]
                            last = pe.matmul(o, q_t[:, k * C:k * C + C], u, start=False, stop=True)
                last.then_inc(at_ps, 1)

            def w1_mm(f, par, s):
                nb, n = batches(f), chunks(f) * C
                e, b = s // nb, s % nb
                if e == 0:
                    pe.wait_ge(f2_sb, 2 if is_cls(f) else upto(f, 4, 3 + b, 2))
                    pe.wait_ge(f1_lo, upto(f, 2, b + 1, 1))
                if is_cls(f):
                    if s >= 2:
                        pe.wait_ge(hid_sb, s - 1)
                else:
                    pe.wait_ge(hid_sb, upto(f, 16, s - 1, 8))
                w = slice(e * HID, e * HID + HID)
                pe.matmul(zb[s % 2][:, 0:n], w1_hi[:, w], f1_t[par][:, b * NT:b * NT + n], start=True, stop=False)
                pe.matmul(zb[s % 2][:, 0:n], w1_lo[:, w], f2_t[par][:, b * NT:b * NT + n], start=False, stop=True)\
                  .then_inc(hid_ps, 1)

            def w2_mm(f, par, j, b):
                nb, n = batches(f), chunks(f) * C
                s0, s1 = 2 * j * nb + b, (2 * j + 1) * nb + b
                if j == 0:
                    if not is_cls(f):
                        pe.wait_ge(y_ev, whole(f - 1, 2, 1))
                    pe.matmul(yb[b][:, 0:n], b2_t[:, :], f2_t[par][:, b * NT:b * NT + n], start=True, stop=False)
                pe.wait_ge(hid_sb, upto(f, 16, s1 + 1, 8))
                pe.matmul(yb[b][0:64, 0:n], w2_t[:, 2 * j * D:2 * j * D + D], hid[:, s0 % 8, 0:n],
                          start=False, stop=j == 3)
                last = pe.matmul(yb[b][64:128, 0:n], w2_t[:, (2 * j + 1) * D:(2 * j + 2) * D],
                                 hid[:, s1 % 8, 0:n], start=False, stop=j == 3)
                if j == 3:
                    last.then_inc(y_ps, 1)

            def yt_mm(f, tiles):
                if not is_cls(f):
                    pe.wait_ge(o_done, whole(f - 1, 2, 1))
                if tiles is not None:
                    pe.wait_ge(tap_mul, TAPS * tiles)
                for b in range(batches(f)):
                    pe.wait_ge(y_ev, upto(f, 2, b + 1, 1))
                    for c in range(chunks(f)):
                        last = pe.transpose(mb[2 + b][:, c * C:c * C + C], y_sb[:, b, c * C:c * C + C], ident[:, :])
                    last.then_inc(yt_ps, 1)

            pe.wait_ge(ld_tok, 80)
            pe.wait_ge(ld_band, 16)
            pe.wait_ge(guards, 8)
            pe.wait_ge(conv2_ready, 1)

            def add_mm(q, slot, j, used):
                lo, hi = w_range(TAP_ORDER[j])
                if j == 0 and used is not None:
                    pe.wait_ge(part_sum, used)
                pe.wait_ge(tap_mul, q * TAPS + j + 1)
                pe.matmul(part_bank[slot][:, :].rearrange("p (r w) -> p r w", w=IMG)[:, :, lo:hi], ident[:, :],
                          prod[:, j, :].rearrange("p (r w) -> p r w", w=IMG)[:, :, lo:hi],
                          start=j == 0, stop=j == PE_ADDS - 1).then_inc(pe_sum, 1)

            def first_tile(q, slot, after_first=True, used=None, last=False):
                nb = len(tap_bank)
                for j in range(TAPS):
                    if j >= nb:
                        before = q * TAPS + j - nb + 1
                    elif after_first:
                        before = (q - 1) * TAPS + (j + nb + 1 if j + nb < TAPS else j + 1)
                    else:
                        before = None
                    tap_mm(q, slot, j, tap_bank[j % nb], before)
                    if j >= nb:
                        add_mm(q, slot, j - nb, used)
                    if j == nb - 1 and not last:
                        pe.wait_ge(relu_done, 2 * q + 2)
                        conv1_mm(q + 1, 0, q + 1, yb[0])

            assert PE_ADDS == TAPS - len(tap_bank)
            conv1_mm(0, 0, 0, yb[0])
            first_tile(0, 0, after_first=False)
            pe.wait_ge(ld_x[0], 16)
            first_tile(1, 1)
            with pe.Fori(1, TURNS // 2 - 1) as i:
                first_tile(2 * i, 0, used=2 * i - 1)
                first_tile(2 * i + 1, 1, used=2 * i)
            first_tile(TURNS - 2, 0, used=TURNS - 3)
            first_tile(TURNS - 1, 1, used=TURNS - 2, last=True)
            pe.wait_ge(ld_x[1], 16)
            pe.wait_ge(att_w, 1)
            pe.wait_ge(tap_mul, TURNS * TAPS)
            pe.wait_ge(part_sum, TURNS)
            z_mm(0)

            def body(f, fp, tile):
                n, t, m, q = f + 1, f + 2, f + 3, f + 10
                nb = batches(f)

                def slot(s, w1=True, w2=True):
                    if not is_turn(f):
                        return
                    if w1 and s % 2 < nb:
                        w1_mm(f, fp, s if nb == 2 else s // 2)
                    if is_turn(t):
                        if w2 and s >= 4 and s % 4 < nb:
                            w2_mm(f, fp, s // 4 - 1, s % 4)
                    elif w2 and s >= 4 and s % 2 == 0:
                        w2_mm(f, fp, s // 4 - 1, s % 4 // 2)

                def tap(j):
                    if tile:
                        tap_mm(q, fp, j, mb[3 - j % 2], None if j < 2 else q * TAPS + j - 1)

                slot(0)
                slot(1)
                if is_turn(f - 1):
                    yt_mm(f - 1, q if tile or isinstance(f, int) and f == 6 else None)
                slot(2)
                slot(3)
                if is_turn(t):
                    q_mm(t)
                slot(4)
                if is_turn(t):
                    kv_mm(t, 0)
                    if not is_cls(t):
                        kv_mm(t, 1)
                if tile:
                    if is_turn(f - 1):
                        pe.wait_ge(o_done, upto(f - 1, 2, 1, 1))
                    else:
                        pe.wait_ge(tap_mul, q * TAPS)
                    conv1_mm(q, 1, f + 2, mb[2])
                slot(5)
                if is_turn(t) and not is_cls(t):
                    kv_mm(t, 2)
                    kv_mm(t, 3)
                slot(6)
                if is_turn(n):
                    gt_mm(n, t)
                if tile and is_turn(f - 1):
                    pe.wait_ge(o_done, whole(f - 1, 2, 1))
                tap(0)
                tap(1)
                slot(7)
                slot(8)
                tap(2)
                if is_turn(t):
                    kt_mm(t, 0)
                slot(9, w2=False)
                if is_turn(n):
                    if is_cls(n):
                        pe.wait_ge(ffn_w, 1)
                    gate_mm(n, 1 - fp)
                tap(3)
                slot(9, w1=False)
                if is_turn(t) and not is_cls(t):
                    kt_mm(t, 1)
                slot(10)
                if is_turn(t):
                    for b in range(batches(t)):
                        score_mm(t, b)
                slot(11)
                slot(12)
                if is_turn(n):
                    f2_mm(n, t)
                tap(4)
                tap(5)
                if is_turn(t):
                    du_mm(t)
                slot(13)
                slot(14)
                tap(6)
                if is_turn(t):
                    at_mm(t, n)
                tap(7)
                slot(15)
                tap(8)
                if is_turn(f):
                    w2_mm(f, fp, 3, 0)
                if is_turn(m, 1):
                    z_mm(m)
                if is_turn(f) and nb == 2:
                    w2_mm(f, fp, 3, 1)

            all_bodies(pe, body)

        @block.vector
        def _(dve):
            made = [0, None, 0]

            def step(ins):
                ins.then_inc(vec_steps, 1)
                made[2] += 1

            def settled():
                if made[1] is None:
                    dve.wait_ge(vec_steps, made[0] + made[2])
                else:
                    i, per = made[1]
                    dve.wait_ge(vec_steps, i * per + (made[0] + made[2]))

            def flush():
                made[0] += made[2]
                made[2] = 0

            for y in y_st:
                step(dve.memset(y[96:128, :].bitcast(F32), 0.0))
            settled()
            for y in y_st:
                dve.memset(y[96:98, :].bitcast(F32), 1.0).then_inc(guards, 1)
            dve.wait_ge(ld_tok, 80)
            w = c2[:, 0, :]
            hi, lo = c2[:, 1, :].bitcast(F32R), c2[:, 2, :]
            step(dve.tensor_copy(hi, w))
            dve.wait_ge(bn_scale, 1)
            step(dve.tensor_tensor(bn_s[:, 1:2], bn_s[:, 1:2], bn_t[:, 1:2], ALU.mult))
            step(dve.tensor_tensor(bn_s[:, 3:4], bn_t[:, 0:1], bn_t[:, 3:4], ALU.subtract))
            settled()
            step(dve.tensor_tensor(lo, w, hi.bitcast(F32), ALU.subtract))
            dve.scalar_tensor_tensor(bn_s[:, 2:3], bn_s[:, 3:4], bn_s[:, 1:2], bn_t[:, 2:3], ALU.mult, ALU.add)\
               .then_inc(bn_bias, 1)
            settled()
            step(dve.tensor_scalar(lo, lo, selt[:, 1:2], None, ALU.mult))
            settled()
            step(dve.scalar_tensor_tensor(c2[:, 3, :], hi.bitcast(F32), selt[:, 0:1], lo, ALU.mult, ALU.add))
            settled()
            dve.tensor_tensor(conv2_t[:, :, :], c2[:, 3, :].unsqueeze(2).broadcast_to([P, TAPS, P]),
                              mask_cols[:, :].unsqueeze(1).broadcast_to([P, TAPS, P]), ALU.mult)\
               .then_inc(conv2_ready, 1)

            def y_low(q, slot):
                y = y_st[slot][32:64, :]
                dve.wait_ge(relu_done, 2 * q + 2)
                dve.tensor_tensor(y, y_f[32:64, :], y.bitcast(F32), ALU.subtract).then_inc(ylo_done, 1)

            def tap(q, j, pair, g, dst, bank):
                k = TAP_ORDER[j]
                di = k // 3 - 1
                lo_, hi_ = w_range(k)
                dj = k % 3 - 1
                img = ximg[pair][:, bass.ds((g * ROWS + 1 + di) * IMG, ROWS * IMG)]\
                    .rearrange("p (r w) -> p r w", w=IMG)[:, :, lo_ + dj:hi_ + dj]
                wt = bank[:, :].rearrange("p (r w) -> p r w", w=IMG)[:, :, lo_:hi_]
                dve.wait_ge(tap_bc, q * TAPS + j + 1)
                dve.tensor_tensor(dst.rearrange("p (r w) -> p r w", w=IMG)[:, :, lo_:hi_], wt, img, ALU.mult)\
                   .then_inc(tap_mul, 1)

            def first_tile(q, slot, after_first=True, last=False):
                for j in range(TAPS):
                    if after_first:
                        if j < PE_ADDS:
                            dve.wait_ge(pe_sum, (q - 1) * PE_ADDS + (j + 1))
                        else:
                            dve.wait_ge(pool_sum, pool_adds(q - 1, True) + (j - PE_ADDS + 1))
                    tap(q, j, 0, q, prod[:, j, :], tap_bank[j % len(tap_bank)])
                    if j == TAPS - 4 and not last:
                        y_low(q + 1, 1 - slot)

            def split(src, hi, lo):
                step(dve.tensor_copy(hi, src))
                settled()
                step(dve.tensor_tensor(lo, src, hi.bitcast(F32), ALU.subtract))

            def bc(stat, width):
                return stat[:, 0:width].unsqueeze(2).broadcast_to([P, width, D])

            def norm_centre(src, width):
                step(dve.tensor_reduce(st[:, 0, 0:width], src, AX.X, ALU.add))
                settled()
                step(dve.tensor_scalar(st[:, 1, 0:width], st[:, 0, 0:width], 1.0 / D, None, ALU.mult))
                settled()
                dve.tensor_tensor(xm[:, 0:width, :], src, bc(st[:, 1, :], width), ALU.subtract)\
                   .then_inc(centred, 1)

            def norm_sum(n, width):
                dve.wait_ge(squared, n + 1)
                step(dve.tensor_reduce(st[:, 2, 0:width], sq[:, 0:width, :], AX.X, ALU.add))
                settled()
                dve.tensor_scalar(st[:, 3, 0:width], st[:, 2, 0:width], 1.0 / D, LN_EPS, ALU.mult, ALU.add)\
                   .then_inc(sumsq, 1)

            def norm_scale(n, width, z):
                dve.wait_ge(rstd, n + 1)
                dve.wait_ge(centred, n + 1)
                dve.tensor_tensor(z[:, 0:width, :], xm[:, 0:width, :], bc(st[:, 4, :], width), ALU.mult)\
                   .then_inc(normed, 1)

            def low(dst, bank, n, b, done):
                half, other = slice(D * b, D * b + D), slice(D - D * b, 2 * D - D * b)
                cols = slice(b * NT, b * NT + n)
                dve.tensor_tensor(dst[other, cols], bank[half, 0:n], dst[half, cols].bitcast(F32), ALU.subtract)\
                   .then_inc(done, 1)

            def z_low(t):
                dve.wait_ge(z_hi, whole(t, 2, 1))
                for b in range(batches(t)):
                    low(z_t, mb[0], chunks(t) * C, b, z_lo)

            def f1_low(n, par):
                dve.wait_ge(f1_hi, whole(n, 2, 1))
                for b in range(batches(n)):
                    low(f1_t[par], mb[1], chunks(n) * C, b, f1_lo)

            def q_rot(t):
                n = chunks(t) * C
                for b in range(batches(t)):
                    dve.wait_ge(q_ps, upto(t, 2, b + 1, 1))
                    tab = tabc_t[:, 0:C] if is_cls(t) else tabq_t[:, bass.ds(place(t) * NT, NT)]
                    dve.tensor_tensor(q_t[:, b * NT:b * NT + n], mb[1 - b][:, 0:n], tab, ALU.mult).then_inc(q_sb, 1)

            def k_rotate(t, u):
                n = min(2, chunks(t))
                dve.wait_ge(kv_ps, upto(t, 4, u + 1, 1))
                kv = kv_bank[u][:, 0:n * 192].rearrange("p (c k) -> p c k", k=192)[:, :, 0:128]
                if batches(t) == 1:
                    tab = tabc_t[:, C:2 * C]
                else:
                    tab = tabk_t[:, bass.ds(place(t) * NT + 2 * (u % 2) * C, 2 * C)]
                dve.tensor_tensor(km[:, 2 * u:2 * u + n, :], kv, tab.rearrange("p (c k) -> p c k", k=C),
                                  ALU.mult).then_inc(k_mul, 1)

            def k_double(t, b):
                n = chunks(t)
                dve.wait_ge(k_mul, upto(t, 4, 2 * b + 2, 1) if n == CPT else 1)
                src = km[:, CPT * b:CPT * b + n, :]
                dst = kd[:, CPT * b:CPT * b + n, :].rearrange("p c (r d) -> p c r d", r=2)
                one = src[:, :, 0:D].unsqueeze(2).broadcast_to([P, n, 2, D])
                two = src[:, :, D:2 * D].unsqueeze(2).broadcast_to([P, n, 2, D])
                dve.tensor_tensor(dst, one, two, ALU.add).then_inc(k_rot, 1)

            def probs(t, b):
                n = chunks(t)
                dve.wait_ge(sc_ps, upto(t, 2, b + 1, 1))
                mask = causal_t if batches(t) == 2 else ident
                dve.tensor_tensor(prob[:, b * NT:b * NT + n * C].rearrange("p (c k) -> p c k", k=C),
                                  mb[b][:, 0:n * C].rearrange("p (c k) -> p c k", k=C),
                                  mask[:, :].unsqueeze(1).broadcast_to([P, n, C]), ALU.mult).then_inc(prob_sb, 1)

            DECAY = GAMMA ** C
            du = mb[1][:, :].rearrange("p (b c d) -> p c b d", b=2, c=CPT)

            def states(t):
                if isinstance(t, int) and t % TURNS == 1:
                    for b in range(2):
                        step(dve.tensor_copy(u_car[:, b, :], u_cls[:, :]))
                    settled()
                dve.wait_ge(du_ps, t + 1)
                if is_cls(t):
                    dve.tensor_scalar(u_cls[:, :], mb[1][:, 0:D], GAMMA, None, ALU.mult).then_inc(du_used, 1)
                    return
                for c in range(CPT - 1):
                    prev = u_car[:, :, :] if c == 0 else u_in[:, c, :, :]
                    ins = dve.scalar_tensor_tensor(u_in[:, c + 1, :, :], prev, DECAY, du[:, c], ALU.mult, ALU.add)
                    if c == CPT - 2:
                        ins.then_inc(u_done, 1)
                    else:
                        step(ins)
                        settled()

            def attended(t, par):
                dve.wait_ge(at_ps, t + 1)
                width = 1 if is_cls(t) else 8
                if not is_cls(t):
                    dve.wait_ge(h2_kept, t)
                dve.tensor_tensor(h2n[:, 0:width, :], h1[par][:, 0:width, :],
                                  mb[0][:, 0:width * D].rearrange("p (c d) -> p c d", d=D), ALU.add)\
                   .then_inc(h2_done, 1)
                if not is_cls(t):
                    dve.wait_ge(u_done, t)
                    dve.scalar_tensor_tensor(u_car[:, :, :], u_in[:, CPT - 1, :, :], DECAY, du[:, CPT - 1],
                                             ALU.mult, ALU.add).then_inc(du_used, 1)

            def gates(t):
                n = 8 if batches(t) == 2 else 1
                dve.wait_ge(gate_ps, t + 1)
                ps = mb[1][:, 0:n * 16].rearrange("p (c e) -> p c e", e=16)
                g, ge, left, one1, one2 = (gs[:, i, 0:n, :] for i in range(5))
                best, pick = gm[:, 0, 0:n], gm[:, 1, 0:n]

                def wide(x):
                    return x.unsqueeze(2).broadcast_to([P, n, E])

                step(dve.tensor_tensor(g, ps[:, :, 0:E], bg_t[:, :].unsqueeze(1).broadcast_to([P, n, E]), ALU.add))
                settled()
                dve.tensor_tensor(g, g, ps[:, :, E:2 * E], ALU.add).then_inc(gate_read, 1)
                dve.wait_ge(gate_read, t + 1)
                for one in (one1, one2):
                    step(dve.tensor_reduce(best, g, AX.X, ALU.max))
                    settled()
                    step(dve.tensor_tensor(ge, g, wide(best), ALU.is_ge))
                    settled()
                    step(dve.tensor_tensor(ge, ge, order_t[:, :].unsqueeze(1).broadcast_to([P, n, E]), ALU.mult))
                    settled()
                    step(dve.tensor_reduce(pick, ge, AX.X, ALU.max))
                    settled()
                    step(dve.tensor_tensor(one, ge, wide(pick), ALU.is_equal))
                    settled()
                    if one is one1:
                        step(dve.scalar_tensor_tensor(g, one, -3.0e38, g, ALU.mult, ALU.add))
                        settled()
                step(dve.tensor_tensor(left, one1, one2, ALU.add))
                settled()
                if not is_cls(t):
                    dve.wait_ge(f2_ps, t)
                step(dve.tensor_scalar(aux[:, 0:n, 0:E], left, -1.0, 1.0, ALU.mult, ALU.add))
                step(dve.tensor_copy(aux[:, 0:n, 10:18], left))
                dve.tensor_copy(aux[:, 0:n, 18:26], left).then_inc(gated, 1)

            def finish(f, par, b):
                if b >= batches(f):
                    return
                n = chunks(f)
                if b == 0 and not is_cls(f):
                    dve.wait_ge(stored_out, 32 * f - 16)
                dve.wait_ge(h2_kept, f + 1)
                dve.wait_ge(yt_ps, upto(f, 2, b + 1, 1))
                y = mb[2 + b][:, 0:n * C].rearrange("p (c k) -> p c k", k=C)
                o = of_batch(o_t, b, n)
                step(dve.tensor_tensor(o, of_batch(h2[par], b, n), y[:, :, 0:D], ALU.add))
                settled()
                dve.tensor_tensor(o, o, y[:, :, D:2 * D], ALU.add).then_inc(o_done, 1)

            dve.wait_ge(ld_h1, 16)
            norm_centre(h1[0][:, 0:1, :], 1)
            norm_sum(ln1(0), 1)
            norm_scale(ln1(0), 1, ztok)

            dve.wait_ge(guards, 8)
            y_low(0, 0)
            first_tile(0, 0, after_first=False)
            first_tile(1, 1)
            dve.wait_ge(ld_att, 48)
            split(qkv_raw[:, :], qkv_hi[:, :], qkv_lo[:, :])
            settled()
            dve.memset(u_cls[:, :], 0.0).then_inc(att_w, 1)
            with dve.Fori(1, TURNS // 2 - 1) as i:
                first_tile(2 * i, 0)
                first_tile(2 * i + 1, 1)
            first_tile(TURNS - 2, 0)
            first_tile(TURNS - 1, 1, last=True)

            def ffn_weights():
                dve.wait_ge(ld_ffn, 112)
                split(wg_raw[:, :], wg_t[:, 0:E], wg_t[:, E:2 * E])
                step(dve.tensor_copy(w1_hi[:, :], w1_raw[:, :]))
                b2h, b2l = b2_tmp[:, 0:P].bitcast(F32R), b2_tmp[:, P:2 * P]
                step(dve.tensor_copy(b2h, b2_raw[:, :]))
                settled()
                step(dve.tensor_copy(w1_raw[:, :].bitcast(F32R), w1_tmp[:, :]))
                step(dve.tensor_tensor(b2l, b2_raw[:, :], b2h.bitcast(F32), ALU.subtract))
                settled()
                step(dve.tensor_tensor(w1_tmp[:, :], w1_tmp[:, :], w1_raw[:, :], ALU.subtract))
                step(dve.tensor_scalar(b2l, b2l, selt[:, 5:6], None, ALU.mult))
                settled()
                step(dve.tensor_scalar(w1_tmp[:, :], w1_tmp[:, :], selt[:, 3:4], None, ALU.mult))
                settled()
                step(dve.scalar_tensor_tensor(b2_t[:, :], b2h.bitcast(F32), selt[:, 4:5], b2l, ALU.mult, ALU.add))
                step(dve.scalar_tensor_tensor(w1_lo[:, :], w1_raw[:, :], selt[:, 2:3], w1_tmp[:, :],
                                              ALU.mult, ALU.add))
                settled()
                dve.memset(u_in[:, 0, :, :], 0.0).then_inc(ffn_w, 1)

            def body(f, fp, tile):
                n, t, m, q = f + 1, f + 2, f + 3, f + 10
                wn = 1 if is_cls(n) else 8

                def mul(j):
                    if tile:
                        if j == 0:
                            dve.wait_ge(pool_sum, pool_adds(q, False))
                            dve.wait_ge(stored_tok[fp], 16 * (q - fp))
                        tap(q, j, 1, f + 2, prod[:, j, :] if j else acc[fp][:, :], mb[3 - j % 2])

                if is_turn(n):
                    dve.wait_ge(h2_done, n + 1)
                    norm_centre(h2n[:, 0:wn, :], wn)
                if is_turn(t):
                    z_low(t)
                if is_turn(n):
                    norm_sum(ln2(n), wn)
                if is_turn(t):
                    if isinstance(t, int) and t == 1:
                        dve.wait_ge(ld_tabs, 32)
                    q_rot(t)
                if is_turn(f - 1):
                    finish(f - 1, 1 - fp, 0)
                if is_turn(n):
                    if not is_cls(n):
                        dve.wait_ge(gt_ps, n)
                    norm_scale(ln2(n), wn, z2tok)
                if is_turn(t):
                    k_rotate(t, 0)
                    if not is_cls(t):
                        k_rotate(t, 1)
                if is_turn(f - 1):
                    finish(f - 1, 1 - fp, 1)
                if is_turn(t):
                    k_double(t, 0)
                if is_turn(t) and not is_cls(t):
                    k_rotate(t, 2)
                    k_rotate(t, 3)
                if tile:
                    y_low(q, fp)
                if is_turn(t) and not is_cls(t):
                    k_double(t, 1)
                mul(0)
                if is_turn(n):
                    f1_low(n, 1 - fp)
                mul(1)
                mul(2)
                if is_turn(n):
                    gates(n)
                mul(3)
                if is_turn(t):
                    for b in range(batches(t)):
                        probs(t, b)
                if is_cls(t):
                    ffn_weights()
                if is_turn(m, 1):
                    dve.wait_ge(ld_h1, whole(m, 32, 16))
                    norm_centre(h1[1 - fp][:, :, :], 8)
                if is_turn(t):
                    states(t)
                mul(4)
                if is_turn(m, 1):
                    norm_sum(ln1(m), 8)
                mul(5)
                if is_turn(m, 1):
                    dve.wait_ge(zt_ps, m)
                    norm_scale(ln1(m), 8, ztok)
                mul(6)
                if is_turn(t):
                    attended(t, fp)
                mul(7)
                mul(8)

            def counted_loop(bodies, tile, per):
                flush()
                with dve.Fori(0, (bodies[1] - bodies[0]) // 2) as i:
                    made[1] = (i, per)
                    body(2 * i + bodies[0], 0, tile)
                    body(2 * i + (bodies[0] + 1), 1, tile)
                    assert made[2] == per, made[2]
                made[1] = None
                made[0], made[2] = made[0] + per * ((bodies[1] - bodies[0]) // 2), 0

            for f in (-2, -1, 0, 1):
                body(f, f % 2, True)
            counted_loop(TILE_LOOP, True, STEPS_TILE)
            for f in (6, 7):
                body(f, f % 2, False)
            counted_loop(LAST_LOOP, False, STEPS_LAST)
            for f in (14, 15, 16, 17):
                body(f, f % 2, False)


STEPS_TILE = 50
STEPS_LAST = 50


def kernel(x, cls_tok, L0_tok_conv1_w, L0_tok_conv1_b, L0_tok_bn_gamma, L0_tok_bn_beta, L0_tok_bn_mean,
           L0_tok_bn_var, L0_tok_conv2_w, L0_tok_conv2_b, L0_attn_W_Q, L0_attn_W_K, L0_attn_W_V, L0_ffn_Wg,
           L0_ffn_bg, L0_ffn_W1, L0_ffn_b1, L0_ffn_W2, L0_ffn_b2):
    import numpy as np
    import concourse.bacc as bacc
    from concourse.bass_utils import run_bass_kernel_spmd

    f = np.float32

    def arr(a):
        return np.ascontiguousarray(a)

    w1c, w2c = arr(L0_tok_conv1_w), arr(L0_tok_conv2_w)
    conv1 = np.zeros((P, 3, 2, CR), f)
    for b in range(2):
        conv1[64 * b:64 * b + 64, :, b, :] = w1c.T[:, None, :]
    bnp = np.stack([np.tile(arr(v), 6) for v in (L0_tok_conv1_b, L0_tok_bn_gamma, L0_tok_bn_beta,
                                                 L0_tok_bn_mean, L0_tok_bn_var)], axis=1)
    conv2 = np.zeros((P, TAPS), f)
    conv2[0:96] = np.tile(w2c.T, (6, 1))
    conv2[96:98] = arr(L0_tok_conv2_b)[None]
    colmask = np.zeros((P, P), f)
    for r in range(3):
        for b in range(2):
            colmask[32 * r + 16 * b:32 * r + 16 * b + 16, 64 * b:64 * b + 64] = 1
    colmask[96:98] = 1
    sel = np.zeros((P, 8), f)
    sel[0:64, 0] = 1
    sel[64:96, 1] = 1
    sel[96, 0] = 1
    sel[97, 1] = 1
    sel[64:73, 2] = 1
    sel[0:64, 3] = 1
    sel[73, 3] = 1
    sel[74:82, 4] = 1
    sel[82:90, 5] = 1

    swap = np.arange(D) ^ 1
    wq, wk, wv = arr(L0_attn_W_Q), arr(L0_attn_W_K), arr(L0_attn_W_V)
    one = np.concatenate([wq, wq[:, swap], wk, wk[:, swap], wv], axis=1)
    wqkv = np.concatenate([one, one], axis=0)

    w1 = arr(L0_ffn_W1).transpose(1, 0, 2).reshape(D, E * HID)
    w1hi = np.concatenate([w1, w1], axis=0)
    w1lo = np.zeros((P, E, HID), f)
    w1lo[0:64] = w1.reshape(D, E, HID)
    for e in range(E):
        w1lo[64 + e, e] = OFF
    w1lo[72:74] = arr(L0_ffn_b1)[None]
    w1lo = w1lo.reshape(P, E * HID)
    w2 = arr(arr(L0_ffn_W2).transpose(1, 0, 2).reshape(HID, E * D))
    b2 = np.zeros((P, P), f)
    b2[74:82, 0:D] = arr(L0_ffn_b2)
    b2[82:90, 0:D] = arr(L0_ffn_b2)
    wg = np.concatenate([arr(L0_ffn_Wg)] * 2, axis=0)
    bg = np.tile(arr(L0_ffn_bg)[None], (P, 1))
    order = np.tile(np.arange(E, 0, -1, dtype=f)[None], (P, 1))

    half = np.arange(0, D, 2, dtype=f)
    inv = (f(1.0) / np.power(f(10000.0), half / f(D))).astype(f)
    pos = np.arange(1, SEQ, dtype=f)
    ang = (pos[:, None] * inv[None, :]).astype(f).astype(np.float64)
    base = ((half + f(0.4 * D)) / f(1.4 * D)).astype(np.float64)
    scale = base[None, :] ** (pos[:, None].astype(np.float64) / 512.0)
    local = (np.arange(HW) % C).astype(np.float64)
    sign = np.where(np.arange(D) % 2 == 0, -1.0, 1.0)
    cos = np.repeat(np.cos(ang), 2, axis=1)
    sin = np.repeat(np.sin(ang), 2, axis=1) * sign
    scale = np.repeat(scale, 2, axis=1)
    q_dec = (GAMMA ** local)[:, None]
    k_dec = (GAMMA ** (C - local))[:, None]
    tabq = arr(np.concatenate([cos * scale * q_dec, sin * scale * q_dec], axis=1).T.astype(f))
    tk = np.concatenate([cos / scale * k_dec, sin / scale * k_dec], axis=1).astype(f)
    tabk = arr(tk.reshape(HW // C, C, 2 * D).transpose(1, 0, 2).reshape(P, HW))
    tabc = np.zeros((P, 2 * C), f)
    tabc[0:64, 0:C] = 1
    tabc[:, C:C + D] = 1
    m = np.arange(C)
    causal = np.where(m[:, None] <= m[None, :], GAMMA ** float(-C), 0.0).astype(f)

    arrays = {
        "x": arr(x).reshape(2, P, HW), "cls": arr(cls_tok).reshape(1, D), "conv1": conv1.reshape(P, 96),
        "bnp": arr(bnp), "conv2": conv2, "colmask": colmask, "sel": sel, "wqkv": arr(wqkv), "w1hi": arr(w1hi),
        "w1lo": w1lo, "w2": w2, "b2": b2, "wg": arr(wg), "bg": arr(bg), "tabq": tabq, "tabk": tabk,
        "tabc": tabc, "causal": causal, "order": arr(order),
    }
    nc = bacc.Bacc("TRN2", target_bir_lowering=False, num_devices=1)
    aps = {n: nc.dram_tensor(n, a.shape, F32, kind="ExternalInput").ap() for n, a in arrays.items()}
    out = nc.dram_tensor("out", (NB, SEQ, D), F32, kind="ExternalOutput").ap()
    build(nc, out=out, **aps)
    r = run_bass_kernel_spmd(nc, [arrays], core_ids=[0])
    return r.results[0]["out"]
```
